# Optimizing a Trainium2 kernel written in Bass

```python
import numpy as np
import jax
import jax.numpy as jnp

def _softmax(x, axis=-1):
    return jax.nn.softmax(x, axis=axis)

def _gelu(x):
    return jax.nn.gelu(x, approximate=True)

def _silu(x):
    return jax.nn.silu(x)

def _sigmoid(x):
    return jax.nn.sigmoid(x)

def _layernorm(x, axis=-1, eps=1e-05):
    m = jnp.mean(x, axis=axis, keepdims=True)
    v = jnp.var(x, axis=axis, keepdims=True)
    return (x - m) / jnp.sqrt(v + eps)

def _scatter_add(tgt, idx, src, axis=0):
    return tgt.at[idx].add(src)

def _segment_sum(src, seg, n):
    return jax.ops.segment_sum(src, seg, n)
kernel_name = 'mk_lm_tower_d1_tok_ids512_r4_45e92a'

def setup_inputs(seed: int=0):
    np.random.seed(seed)
    _w = jnp.asarray

    def _rec_inputs():
        import jax
        import jax.numpy as jnp
        _rk = jax.random.key(seed)
        x = jax.random.randint(jax.random.fold_in(_rk, 1), (32, 128), 0, 12564, jnp.int32)
        return x
    x = _rec_inputs()

    def _L0_tok_setup():
        import jax, jax.numpy as jnp
        import numpy as np
        VOCAB = 50257
        EMB = 128
        key = jax.random.key(seed)
        k1, k2, k3 = jax.random.split(key, 3)
        input_token_ids = jax.random.randint(k1, (8, 1024), 0, VOCAB, dtype=jnp.int64 if jax.config.jax_enable_x64 else jnp.int32)
        W = jax.random.normal(k2, (EMB, VOCAB), dtype=jnp.float32)
        b = jax.random.normal(k3, (EMB,), dtype=jnp.float32)
        return {'input_token_ids': input_token_ids, 'W': W, 'b': b}
    _L0_tok_all = _L0_tok_setup()
    _L0_tok_in = {k: v for k, v in _L0_tok_all.items() if k in ('W', 'b')}
    del _L0_tok_all

    def _L0_attn_setup():
        import jax, jax.numpy as jnp
        import numpy as np
        import math
        D_MODEL = 128
        NUM_HEADS = 8
        LN_EPS = 1e-05
        key = jax.random.key(seed)
        ks = jax.random.split(key, 8)
        B, L, D = (2, 512, D_MODEL)
        x = jax.random.normal(ks[0], (B, L, D), dtype=jnp.float32)
        s = 0.02
        return {'x': x, 'W_qkv': jax.random.normal(ks[1], (D, 3 * D), dtype=jnp.float32) * s, 'b_qkv': jnp.zeros((3 * D,), dtype=jnp.float32), 'W_out': jax.random.normal(ks[2], (D, D), dtype=jnp.float32) * s, 'b_out': jnp.zeros((D,), dtype=jnp.float32), 'decay_logits': jnp.zeros((NUM_HEADS,), dtype=jnp.float32), 'ln_g': jnp.ones((D,), dtype=jnp.float32), 'ln_b': jnp.zeros((D,), dtype=jnp.float32)}
    _L0_attn_all = _L0_attn_setup()
    _L0_attn_in = {k: v for k, v in _L0_attn_all.items() if k in ('W_qkv', 'b_qkv', 'W_out', 'b_out', 'decay_logits', 'ln_g', 'ln_b')}
    del _L0_attn_all

    def _L0_ffn_setup():
        import jax, jax.numpy as jnp
        import numpy as np
        H = 128
        I = 256
        E = 32
        K = 2
        key = jax.random.key(seed)
        ks = jax.random.split(key, 9)
        s = 0.02
        return {'hidden_states': jax.random.normal(ks[0], (2, 1024, H), dtype=jnp.float32), 'Wgate': jax.random.normal(ks[1], (H, E), dtype=jnp.float32) * s, 'bgate': jnp.zeros((E,), dtype=jnp.float32), 'Wg': jax.random.normal(ks[2], (E, H, I), dtype=jnp.float32) * s, 'bg': jnp.zeros((E, I), dtype=jnp.float32), 'Wu': jax.random.normal(ks[3], (E, H, I), dtype=jnp.float32) * s, 'bu': jnp.zeros((E, I), dtype=jnp.float32), 'Wd': jax.random.normal(ks[4], (E, I, H), dtype=jnp.float32) * s, 'bd': jnp.zeros((E, H), dtype=jnp.float32)}
    _L0_ffn_all = _L0_ffn_setup()
    _L0_ffn_in = {k: v for k, v in _L0_ffn_all.items() if k in ('Wgate', 'bgate', 'Wg', 'bg', 'Wu', 'bu', 'Wd', 'bd')}
    del _L0_ffn_all
    return {'x': x, 'L0_tok_W': _L0_tok_in['W'], 'L0_tok_b': _L0_tok_in['b'], 'L0_attn_W_qkv': _L0_attn_in['W_qkv'], 'L0_attn_b_qkv': _L0_attn_in['b_qkv'], 'L0_attn_W_out': _L0_attn_in['W_out'], 'L0_attn_b_out': _L0_attn_in['b_out'], 'L0_attn_decay_logits': _L0_attn_in['decay_logits'], 'L0_attn_ln_g': _L0_attn_in['ln_g'], 'L0_attn_ln_b': _L0_attn_in['ln_b'], 'L0_ffn_Wgate': _L0_ffn_in['Wgate'], 'L0_ffn_bgate': _L0_ffn_in['bgate'], 'L0_ffn_Wg': _L0_ffn_in['Wg'], 'L0_ffn_bg': _L0_ffn_in['bg'], 'L0_ffn_Wu': _L0_ffn_in['Wu'], 'L0_ffn_bu': _L0_ffn_in['bu'], 'L0_ffn_Wd': _L0_ffn_in['Wd'], 'L0_ffn_bd': _L0_ffn_in['bd']}

def reference(x, L0_tok_W, L0_tok_b, L0_attn_W_qkv, L0_attn_b_qkv, L0_attn_W_out, L0_attn_b_out, L0_attn_decay_logits, L0_attn_ln_g, L0_attn_ln_b, L0_ffn_Wgate, L0_ffn_bgate, L0_ffn_Wg, L0_ffn_bg, L0_ffn_Wu, L0_ffn_bu, L0_ffn_Wd, L0_ffn_bd):
    import jax
    import jax.numpy as jnp

    def _L0_tok_ref(input_token_ids, W, b):
        import jax, jax.numpy as jnp
        import numpy as np
        VOCAB = 50257
        EMB = 128
        scale = jnp.asarray(EMB, W.dtype) ** 0.5
        emb = jnp.take(W.T, input_token_ids, axis=0)
        return (emb + b) * scale

    def _L0_attn_ref(x, W_qkv, b_qkv, W_out, b_out, decay_logits, ln_g, ln_b):
        import jax, jax.numpy as jnp
        import numpy as np
        import math
        D_MODEL = 128
        NUM_HEADS = 8
        LN_EPS = 1e-05
        B, L, D = x.shape
        H = NUM_HEADS
        E = D // H
        qkv = x @ W_qkv + b_qkv
        q, k, v = jnp.split(qkv, 3, axis=-1)
        q = q.reshape(B, L, H, E)
        k = k.reshape(B, L, H, E)
        v = v.reshape(B, L, H, E)
        q = (jax.nn.elu(q) + 1.0) / math.sqrt(E)
        k = jax.nn.elu(k) + 1.0
        lam = 0.99 + 0.01 * jax.nn.sigmoid(decay_logits)
        lam = lam.reshape(1, 1, H, 1)
        idx = jnp.arange(L, dtype=jnp.float32).reshape(1, L, 1, 1)
        decay_k = lam ** (-idx)
        decay_q = lam ** idx
        k_d = k * decay_k
        kv = jnp.einsum('blhe,blhf->blhef', k_d, v)
        mem = jnp.cumsum(kv, axis=1)
        k_sum = jnp.cumsum(k_d, axis=1)
        q_d = q * decay_q
        num = jnp.einsum('blhe,blhef->blhf', q_d, mem)
        den = jnp.einsum('blhe,blhe->blh', q_d, k_sum)[..., None] + 1e-06
        out = (num / den).reshape(B, L, D)
        out = out @ W_out + b_out
        mu = jnp.mean(out, axis=-1, keepdims=True)
        var = jnp.var(out, axis=-1, keepdims=True)
        return (out - mu) / jnp.sqrt(var + LN_EPS) * ln_g + ln_b

    def _L0_ffn_ref(hidden_states, Wgate, bgate, Wg, bg, Wu, bu, Wd, bd):
        import jax, jax.numpy as jnp
        import numpy as np
        H = 128
        I = 256
        E = 32
        K = 2
        B, S, Hs = hidden_states.shape
        x = hidden_states.reshape(-1, Hs)
        probs = jax.nn.softmax(x @ Wgate + bgate, axis=-1)
        router_w, sel = jax.lax.top_k(probs, K)
        comb = (jax.nn.one_hot(sel, E, dtype=x.dtype) * router_w[..., None]).sum(axis=1)

        def body(acc, xs):
            Wg_e, bg_e, Wu_e, bu_e, Wd_e, bd_e, w_e = xs
            h = jax.nn.silu(x @ Wg_e + bg_e) * (x @ Wu_e + bu_e)
            acc = acc + w_e[:, None] * (h @ Wd_e + bd_e)
            return (acc, None)
        acc0 = jnp.zeros_like(x)
        acc, _ = jax.lax.scan(body, acc0, (Wg, bg, Wu, bu, Wd, bd, comb.T))
        return acc.reshape(B, S, Hs)
    h = _L0_tok_ref(x, L0_tok_W, L0_tok_b)
    h = h + _L0_attn_ref(_layernorm(h, axis=-1), L0_attn_W_qkv, L0_attn_b_qkv, L0_attn_W_out, L0_attn_b_out, L0_attn_decay_logits, L0_attn_ln_g, L0_attn_ln_b)
    h = h + _L0_ffn_ref(_layernorm(h, axis=-1), L0_ffn_Wgate, L0_ffn_bgate, L0_ffn_Wg, L0_ffn_bg, L0_ffn_Wu, L0_ffn_bu, L0_ffn_Wd, L0_ffn_bd)
    return h

_drawn_inputs = setup_inputs


def setup_inputs(seed=0):
    import zlib

    import numpy as np

    out = dict(_drawn_inputs(seed))
    spreads = {'L0_attn_b_qkv': (0.0, 0.52),
     'L0_attn_b_out': (0.0, 0.1),
     'L0_attn_decay_logits': (0.0, 2.0),
     'L0_attn_ln_g': (1.0, 0.6),
     'L0_attn_ln_b': (0.0, 0.8),
     'L0_ffn_bgate': (0.0, 0.8),
     'L0_ffn_bg': (0.0, 0.8),
     'L0_ffn_bu': (0.0, 0.8),
     'L0_ffn_bd': (0.0, 2.0)}
    factors = {'L0_attn_W_qkv': 2.828,
     'L0_ffn_Wgate': 8.0,
     'L0_ffn_Wg': 8.0,
     'L0_ffn_Wu': 8.0,
     'L0_ffn_Wd': 8.0}
    for name, (base, spread) in spreads.items():
        noise = np.random.default_rng([zlib.crc32(name.encode()), seed]).standard_normal(out[name].shape)
        drawn = base * np.exp(spread * noise) if base else spread * noise
        out[name] = jnp.asarray(drawn.astype(out[name].dtype))
    for name, factor in factors.items():
        out[name] = (out[name] * factor).astype(out[name].dtype)
    return out
```

```python
from contextlib import ExitStack

import concourse.bass as bass
from concourse import mybir

F32 = mybir.dt.float32
BF16 = mybir.dt.bfloat16
I32 = mybir.dt.int32
U32 = mybir.dt.uint32
ALU = mybir.AluOpType
ACT = mybir.ActivationFunctionType
AXX = mybir.AxisListType.X
NOT_EQUAL = ALU.not_equal

P = 128
SEQS = 32
D = 128
HEADS = 8
HD = D // HEADS
E = 32
FF = 256
TOP = 2
TOK = SEQS * P
U = 2
UNITS = SEQS // U
W = U * P
REG = TOK + P
TILES = TOP * TOK // P + E
ROW = D + 2
DUMMY = E * REG
SKIP = 1 << 20
LN_EPS = 1e-5
DEN_EPS = 1e-6
EMB_SCALE = float(D) ** 0.5
ROW_TOKB, ROW_BV, ROW_BOUT, ROW_LNG, ROW_LNB, ROW_BGATE = (D * i for i in range(6))
ROWS_N = 5 * D + E
BIAS_N = 2 * FF + D


def build(nc, ids, wt, rows, bqk, decay, wqkv, wout, wgate, wgu, wd, ebias, out):
    ctx = ExitStack()
    with ctx:
        def sb(name, shape, dt=F32):
            return ctx.enter_context(nc.sbuf_tensor(name, shape, dt))

        def ps(name, shape, dt=F32):
            return ctx.enter_context(nc.psum_tensor(name, shape, dt))

        def sem(name):
            return ctx.enter_context(nc.semaphore(name))

        xs_dram = nc.dram_tensor("dispatched_rows", [E * REG + P, ROW], F32, kind="Internal").ap()
        y_dram = nc.dram_tensor("expert_rows", [TOP * TOK, D], F32, kind="Internal").ap()

        wgu_sb = sb("wgu_sb", [P, E * 2 * FF])
        wd_sb = sb("wd_sb", [P, E * 2 * D])
        wqkv_sb = sb("wqkv_sb", [P, 3 * D])
        wout_sb = sb("wout_sb", [P, D])
        wgate_sb = sb("wgate_sb", [P, E])
        rows_sb = sb("rows_sb", [P, ROWS_N])
        bqk_sb = sb("bqk_sb", [P, 2])
        dl_sb = sb("dl_sb", [P, 1])
        lam = sb("lam", [P, 2])
        ids_sb = sb("ids_sb", [P, SEQS], U32)
        ids_now = sb("ids_now", [P, 2, U], U32)
        embb = sb("embb", [P, D])
        decq = sb("decq", [P, P])
        deck = sb("deck", [P, P])
        dec_even = sb("dec_even", [P, P])
        dec_odd = sb("dec_odd", [P, P])
        causal = sb("causal", [P, P])
        ident = sb("ident", [P, P])
        tri = sb("tri", [P, P], BF16)
        ones_bf = sb("ones_bf", [P, P], BF16)
        den_w = sb("den_w", [P, 2, 2 * HD])
        par_i = sb("par_i", [P, 1], I32)
        par = sb("par", [P, 2])
        iota_e = sb("iota_e", [P, E])
        eoff = sb("eoff", [P, E])
        tokid = sb("tokid", [P, TOP, SEQS], I32)
        pad_rows = sb("pad_rows", [P, ROW])
        eb3 = sb("eb3", [P, BIAS_N])
        ebr = sb("ebr", [P, BIAS_N])
        ebm = sb("ebm", [P, BIAS_N], BF16)
        bias_bf = sb("bias_bf", [P, BIAS_N], BF16)
        selp = sb("selp", [P, E], BF16)
        sel = sb("sel", [P, E, P], BF16)
        eps_ln = sb("eps_ln", [P, 1])
        eps_den = sb("eps_den", [P, 1])
        h2 = sb("h2", [P, SEQS, D])

        emb = sb("emb", [P, 2, U, D])
        h = sb("h", [P, 2, U, D])
        st1 = sb("st1", [P, U, 6])
        mv1 = sb("mv1", [P, U, 2])
        ln1 = sb("ln1", [P, U])
        rs1 = sb("rs1", [P, U])
        xn = sb("xn", [P, U, D])
        xnT = sb("xnT", [P, W])
        relu_qk = sb("relu_qk", [P, 2, W])
        exp_qk = sb("exp_qk", [P, 2, W])
        qk = sb("qk", [P, 2, W])
        kd = sb("kd", [P, 2, W])
        qeo = sb("qeo", [P, 2, U, 2, P])
        veo = sb("veo", [P, 2, U, 2, D])
        sm = sb("sm", [P, 4, U * 2, P])
        den_sb = sb("den_sb", [P, W])
        rec = sb("rec", [P, W])
        oT = sb("oT", [P, W])
        ao = sb("ao", [P, U, D])
        hlb = sb("hlb", [P, U, D])
        st2 = sb("st2", [P, U, 6])
        mv2 = sb("mv2", [P, U, 2])
        ln2 = sb("ln2", [P, U])
        rs2 = sb("rs2", [P, U])
        aog = sb("aog", [P, U, D])
        st3 = sb("st3", [P, U, 6])
        mv3 = sb("mv3", [P, U, 2])
        ln3 = sb("ln3", [P, U])
        rs3 = sb("rs3", [P, U])
        rr = sb("rr", [P, 2, TOP, U, ROW])
        x2T = sb("x2T", [P, W])
        lg = sb("lg", [P, U, E])
        mx = sb("mx", [P, U, 8])
        mi = sb("mi", [P, U, 8], U32)
        mif = sb("mif", [P, U, TOP])
        ls = sb("ls", [P, U, E + TOP])
        es = sb("es", [P, U, E + TOP])
        ssum = sb("ssum", [P, U])
        rsum = sb("rsum", [P, U])
        mk = sb("mk", [P, TOP, U, E])
        msum = sb("msum", [P, U, E], BF16)
        cum = sb("cum", [P, 2, E], BF16)
        mpair = sb("mpair", [P, E], BF16)
        rank = sb("rank", [P, U, E])
        slotp = sb("slotp", [P, TOP, U, E])
        slotf = sb("slotf", [P, TOP, U])
        slot = sb("slot", [P, 2, TOP, U], U32)

        cnt = sb("cnt", [P, E])
        cnt_i = sb("cnt_i", [P, E], I32)
        nt_i = sb("nt_i", [P, E], I32)
        ntf = sb("ntf", [P, E])
        onesf = sb("onesf", [P, E])
        endt = sb("endt", [P, E])
        tileno = sb("tileno", [P, 1])
        passed = sb("passed", [P, E])
        passn = sb("passn", [P, E])
        tab = sb("tab", [P, 4])
        padrow_f = sb("padrow_f", [P, E])
        padrow = sb("padrow", [P, E], I32)
        tab_e = sb("tab_e", [1, TILES], I32)
        tab_b = sb("tab_b", [1, TILES], I32)

        R = 8
        xs = sb("xs", [P, R, ROW])
        widx = sb("widx", [P, R, 2])
        xT = sb("xT", [P, R, P])
        sg = sb("sg", [P, 2, FF])
        hh = sb("hh", [P, 2, FF])
        hT = sb("hT", [P, 2, FF])
        ysb = sb("ysb", [P, R, D])
        CB = 4
        ya = sm[:, 0:2, :, :].rearrange("p b c d -> p b (c d)")
        yb = sm[:, 2:4, :, :].rearrange("p b c d -> p b (c d)")

        bank = [ps(f"bank{i}", [P, 512]) for i in range(8)]
        sc_ps = bank[0:4]
        xnT_ps = bank[4][:, 0:W]
        v_ps = bank[4][:, W:2 * W]
        qk_ps = bank[5]
        num_ps = bank[6][:, 0:W]
        den_ps = bank[6][:, W:2 * W]
        ao_ps = bank[6][:, 0:W]
        x2T_ps = bank[7][:, 0:W]
        lg_ps = bank[7][:, W:W + U * E]
        rk_ps = bank[7][:, W + U * E:W + 2 * U * E]
        cnt_ps = bank[7][:, W + 2 * U * E:W + 2 * U * E + E]
        tab_ps = bank[5]
        gu_ps = [bank[0], bank[1]]
        hT_ps = [bank[2][:, 0:FF], bank[3][:, 0:FF]]
        xT_ps = [bank[4][:, 0:P], bank[5][:, 0:P]]
        y_ps = [bank[6][:, 0:D], bank[7][:, 0:D]]

        ids_in = sem("ids_in")
        small_in = sem("small_in")
        ebias_in = sem("ebias_in")
        experts_in = sem("experts_in")
        pool_const = sem("pool_const")
        dve_const = sem("dve_const")
        act_const = sem("act_const")
        bias_ready = sem("bias_ready")
        ids_staged_first = sem("ids_staged_first")
        ids_staged = [sem(f"ids_staged{b}") for b in range(2)]
        emb_in = [[sem(f"emb_in{b}{s}") for s in range(U)] for b in range(2)]
        h_ready = sem("h_ready")
        st1_ready = sem("st1_ready")
        mv1_ready = sem("mv1_ready")
        ln1_ready = sem("ln1_ready")
        rs1_ready = sem("rs1_ready")
        xn_ready = sem("xn_ready")
        xnT_made = sem("xnT_made")
        xnT_ready = sem("xnT_ready")
        qk_made = sem("qk_made")
        v_made = sem("v_made")
        act_qk = sem("act_qk")
        qk_ready = sem("qk_ready")
        kq_ready = sem("kq_ready")
        v_ready = sem("v_ready")
        sc_made = sem("sc_made")
        sm_ready = sem("sm_ready")
        nd_made = sem("nd_made")
        den_ready = sem("den_ready")
        rec_ready = sem("rec_ready")
        oT_ready = sem("oT_ready")
        ao_made = sem("ao_made")
        ao_ready = sem("ao_ready")
        st2_ready = sem("st2_ready")
        mv2_ready = sem("mv2_ready")
        ln2_ready = sem("ln2_ready")
        rs2_ready = sem("rs2_ready")
        aog_ready = sem("aog_ready")
        h2_ready = sem("h2_ready")
        st3_ready = sem("st3_ready")
        mv3_ready = sem("mv3_ready")
        ln3_ready = sem("ln3_ready")
        rs3_ready = sem("rs3_ready")
        rr0_ready = sem("rr0_ready")
        rr1_ready = [sem(f"rr1_ready{b}") for b in range(2)]
        x2T_made = sem("x2T_made")
        x2T_ready = sem("x2T_ready")
        lg_made = sem("lg_made")
        lg_ready = sem("lg_ready")
        mx_ready = sem("mx_ready")
        mi_ready = sem("mi_ready")
        mif_ready = sem("mif_ready")
        ls_ready = sem("ls_ready")
        es_ready = sem("es_ready")
        ssum_ready = sem("ssum_ready")
        rsum_ready = sem("rsum_ready")
        w_ready = [sem(f"w_ready{b}") for b in range(2)]
        mk_ready = sem("mk_ready")
        msum_ready = sem("msum_ready")
        mpair_ready = sem("mpair_ready")
        cum_ready = sem("cum_ready")
        rk_made = sem("rk_made")
        rank_ready = sem("rank_ready")
        slotp_ready = sem("slotp_ready")
        slotf_ready = sem("slotf_ready")
        slot_ready = [sem(f"slot_ready{b}") for b in range(2)]
        rows_out = [[sem(f"rows_out{b}{c}") for c in range(TOP * U)] for b in range(2)]
        cnt_made = sem("cnt_made")
        tab_step = sem("tab_step")
        tab_made = sem("tab_made")
        tab_ready = sem("tab_ready")
        pads_out = sem("pads_out")
        pads_out_act = sem("pads_out_act")
        xs_in = [sem(f"xs_in{r}") for r in range(R)]
        widx_ready = sem("widx_ready")
        xT_made = sem("xT_made")
        xT_ready = sem("xT_ready")
        gu_made = sem("gu_made")
        sg_ready = sem("sg_ready")
        hh_ready = sem("hh_ready")
        hT_made = sem("hT_made")
        hT_ready = sem("hT_ready")
        y_made = sem("y_made")
        y_ready = [sem(f"y_ready{r}") for r in range(R)]
        y_out = [sem(f"y_out{r}") for r in range(R)]
        ya_in = [sem(f"ya_in{b}") for b in range(2)]
        yb_in = [sem(f"yb_in{b}") for b in range(2)]
        sum1_ready = sem("sum1_ready")
        sum_ready = sem("sum_ready")
        stored = [sem(f"stored{b}") for b in range(2)]

        CONST_POOL = 21

        block = ctx.enter_context(nc.Block())

        def lap(t, q):
            return t + (q // R + 1)

        def stands_first(eng, passed):
            eng.wait_ge(passed, 1)

        def steps(eng, step, first, last):
            n = (last - first) // 2
            if n > 1:
                with eng.Fori(0, n) as t:
                    for k in range(2):
                        step(t * 2 + (first + k), (first + k) % 2)
            else:
                n = 0
            for i in range(first + 2 * n, last):
                step(i, i % 2)

        def skewed(eng, step):
            step(0, 0, True, False, False)
            step(1, 1, True, True, False)
            step(2, 0, True, True, True)
            step(3, 1, True, True, True)
            steps(eng, lambda i, b: step(i, b, True, True, True), 4, UNITS)
            step(UNITS, UNITS % 2, False, True, True)
            step(UNITS + 1, (UNITS + 1) % 2, False, False, True)

        @block.sync
        def _(sp):
            sp.dma_start(ids_sb[:], ids).then_inc(ids_in, 16)
            sp.dma_start(rows_sb[:], rows.rearrange("(a n) -> a n", a=1).broadcast_to([P, ROWS_N])).then_inc(small_in, 16)
            sp.dma_start(bqk_sb[:], bqk).then_inc(small_in, 16)
            sp.dma_start(dl_sb[:], decay).then_inc(small_in, 16)
            sp.dma_start(wqkv_sb[:], wqkv).then_inc(small_in, 16)
            sp.dma_start(wout_sb[:], wout).then_inc(small_in, 16)
            sp.dma_start(wgate_sb[:], wgate).then_inc(small_in, 16)
            for c in range(3):
                sp.dma_start(eb3[32 * c:32 * c + 32, :], ebias).then_inc(ebias_in, 16)
            for c in range(8):
                n = E * 2 * FF // 8
                sp.dma_start(wgu_sb[:, c * n:(c + 1) * n], wgu[:, c * n:(c + 1) * n]).then_inc(experts_in, 16)
            for c in range(4):
                n = E * 2 * D // 4
                sp.dma_start(wd_sb[:, c * n:(c + 1) * n], wd[:, c * n:(c + 1) * n]).then_inc(experts_in, 16)

            sp.wait_ge(pool_const, CONST_POOL)
            sp.dma_start(xs_dram[DUMMY:DUMMY + P, :], pad_rows[:]).then_inc(pads_out, 16)
            sp.wait_ge(tab_ready, 1)
            with sp.Fori(0, E // 2) as e:
                row = sp.value_load(padrow[0:1, bass.ds(e, 1)], min_val=0, max_val=DUMMY)
                sp.dma_start(xs_dram[bass.ds(row, P), :], pad_rows[:]).then_inc(pads_out, 16)
            for b in range(2):
                for c in range(TOP * U):
                    sp.wait_ge(rows_out[b][c], 16 * (UNITS // 2))
            sp.wait_ge(tab_ready, 3)
            sp.wait_ge(pads_out, 16 * (E // 2 + 1))
            sp.wait_ge(pads_out_act, 16 * (E // 2))

            def load_tile(j, r, lap):
                row = sp.value_load(tab_b[0:1, bass.ds(j, 1)], min_val=0, max_val=DUMMY)
                if lap is not None:
                    sp.wait_ge(xT_made, lap)
                    sp.wait_ge(widx_ready, lap)
                sp.dma_start(xs[:, r, :], xs_dram[bass.ds(row, P), :]).then_inc(xs_in[r], 16)

            for r in range(R):
                load_tile(r, r, None)
            with sp.Fori(1, TILES // R) as t:
                for r in range(R):
                    load_tile(t * R + r, r, t * R + (r + 1 - R))

            for r in range(R):
                sp.wait_ge(y_out[r], 16 * (TILES // R))

            y_t = y_dram.rearrange("(k t p) d -> p k t d", k=TOP, p=P)

            def load_pair(n, b, lap):
                if lap is not None:
                    sp.wait_ge(stored[b], lap)
                for k, (dst, arrived) in enumerate(((ya, ya_in), (yb, yb_in))):
                    sp.dma_start(dst[:, b, :].rearrange("p (c d) -> p c d", d=D),
                                 y_t[:, k, bass.ds(n * CB, CB), :]).then_inc(arrived[b], 16)

            for b in range(2):
                load_pair(b, b, None)
            with sp.Fori(1, SEQS // CB // 2) as t:
                for b in range(2):
                    load_pair(t * 2 + b, b, t * 16)
            for b in range(2):
                sp.wait_ge(stored[b], 16 * (SEQS // CB // 2))

        @block.gpsimd
        def _(pool):
            n = [0]

            def made(ins):
                n[0] += 1
                ins.then_inc(pool_const, 1)

            made(pool.memset(ident[:], 0.0))
            made(pool.memset(causal[:], 1.0))
            made(pool.memset(tri[:], 1.0))
            made(pool.memset(ones_bf[:], 1.0))
            made(pool.memset(den_w[:], 0.0))
            made(pool.memset(pad_rows[:], 0.0))
            made(pool.memset(selp[:], 0.0))
            made(pool.iota(par_i[:], [[0, 1]], base=0, channel_multiplier=1))
            made(pool.iota(tokid[:], [[TOK, TOP], [P, SEQS]], base=0, channel_multiplier=1))
            made(pool.iota(iota_e[:], [[1, E]], base=0, channel_multiplier=0, allow_small_or_imprecise_dtypes=True))
            made(pool.iota(eoff[:], [[REG, E]], base=0, channel_multiplier=0, allow_small_or_imprecise_dtypes=True))
            made(pool.iota(tileno[:], [[0, 1]], base=0, channel_multiplier=1, allow_small_or_imprecise_dtypes=True))
            pool.wait_ge(pool_const, n[0])
            made(pool.affine_select(out=ident[:], in_=ident[:], compare_op=NOT_EQUAL, fill=1.0, base=0,
                                    pattern=[[-1, P]], channel_multiplier=1))
            made(pool.affine_select(out=causal[:], in_=causal[:], compare_op=ALU.is_ge, fill=0.0, base=0,
                                    pattern=[[1, P]], channel_multiplier=-1))
            made(pool.affine_select(out=tri[:], in_=tri[:], compare_op=ALU.is_gt, fill=0.0, base=0,
                                    pattern=[[1, P]], channel_multiplier=-1))
            made(pool.memset(den_w[:, 0, 0:HD], 1.0))
            made(pool.memset(den_w[:, 1, HD:2 * HD], 1.0))
            made(pool.iota(pad_rows[:, ROW - 1:ROW].bitcast(I32), [[0, 1]], base=SKIP, channel_multiplier=0))
            for c in range(3):
                made(pool.affine_select(out=selp[:], in_=selp[:], compare_op=NOT_EQUAL, fill=1.0, base=-32 * c,
                                        pattern=[[-1, E]], channel_multiplier=1))
                pool.wait_ge(pool_const, n[0])
            assert n[0] == CONST_POOL

            pool.wait_ge(ids_in, 16)

            def gather(u, b, lap, staged, count):
                if lap is not None:
                    for s in range(U):
                        pool.wait_ge(emb_in[b][s], lap * 16)
                    pool.wait_ge(h_ready, u - 1)
                pool.tensor_copy(ids_now[:, b, :], ids_sb[:, bass.ds(u * U, U)]).then_inc(staged, 1)
                stands_first(pool, pool_const)
                pool.wait_ge(staged, count)
                for s in range(U):
                    pool.indirect_dma_start(emb[:, b, s, :], None, wt,
                                            bass.IndirectOffsetOnAxis(ap=ids_now[:, b, s:s + 1], axis=0))\
                        .then_inc(emb_in[b][s], 16)

            def scatter(b, count):
                stands_first(pool, pool_const)
                pool.wait_ge(slot_ready[b], count)
                pool.wait_ge(w_ready[b], count)
                pool.wait_ge(rr1_ready[b], count)
                for k in range(TOP):
                    for s in range(U):
                        pool.indirect_dma_start(xs_dram, bass.IndirectOffsetOnAxis(ap=slot[:, b, k, s:s + 1], axis=0),
                                                rr[:, b, k, s, :], None).then_inc(rows_out[b][k * U + s], 16)

            gather(0, 0, None, ids_staged_first, 1)
            gather(1, 1, None, ids_staged_first, 2)
            gather(2, 0, 1, ids_staged_first, 3)
            with pool.Fori(1, UNITS // 2 - 1) as t:
                gather(t * 2 + 1, 1, t, ids_staged[1], t)
                scatter(0, t)
                gather(t * 2 + 2, 0, t + 1, ids_staged[0], t)
                scatter(1, t)
            gather(UNITS - 1, 1, UNITS // 2 - 1, ids_staged_first, 4)
            for u in range(UNITS - 4, UNITS):
                scatter(u % 2, u // 2 + 1)

            with pool.Fori(1, TILES // R + 1) as t:
                for r in range(R):
                    stands_first(pool, pool_const)
                    pool.wait_ge(y_ready[r], t)
                    pool.indirect_dma_start(y_dram, bass.IndirectOffsetOnAxis(ap=widx[:, r, 1:2].bitcast(U32), axis=0),
                                            ysb[:, r, :], None, bounds_check=TOP * TOK - 1, oob_is_err=False)\
                        .then_inc(y_out[r], 16)

        @block.scalar
        def _(act):
            act.wait_ge(small_in, 16 * 6)
            nc.scalar.activation(lam[:, 0:1], dl_sb[:], ACT.Exp, scale=-1.0).then_inc(act_const, 1)
            act.wait_ge(dve_const, 1)

            def rstd(var, ln, rs, mv_ready, ln_ready, rs_ready, u):
                act.wait_ge(mv_ready, u + 1)
                nc.scalar.activation(ln[:], var[:, :, 1], ACT.Ln, bias=eps_ln[:, 0:1]).then_inc(ln_ready, 1)
                act.wait_ge(ln_ready, u + 1)
                nc.scalar.activation(rs[:], ln[:], ACT.Exp, scale=-0.5).then_inc(rs_ready, 1)

            def step(i, b, first, second, third):
                if third:
                    rstd(mv3, ln3, rs3, mv3_ready, ln3_ready, rs3_ready, i - 2)
                if first:
                    rstd(mv1, ln1, rs1, mv1_ready, ln1_ready, rs1_ready, i)
                    act.wait_ge(xnT_made, i + 1)
                    nc.scalar.activation(xnT[:], xnT_ps, ACT.Copy).then_inc(xnT_ready, 1)
                if third:
                    act.wait_ge(x2T_made, i - 1)
                    nc.scalar.activation(x2T[:], x2T_ps, ACT.Copy).then_inc(x2T_ready, 1)
                    act.wait_ge(rr0_ready, 2 * i - 2)
                    for s in range(U):
                        ins = nc.scalar.activation(rr[:, b, 1, s, 0:D], rr[:, b, 0, s, 0:D], ACT.Copy)
                    ins.then_inc(rr1_ready[b], 1)
                if second:
                    act.wait_ge(nd_made, i)
                    nc.scalar.activation(den_sb[:], den_ps, ACT.Identity, bias=eps_den[:, 0:1]).then_inc(den_ready, 1)
                if first:
                    act.wait_ge(qk_made, i + 1)
                    if not isinstance(i, int) or i > 0:
                        act.wait_ge(qk_ready, i)
                    for c in range(2):
                        nc.scalar.activation(relu_qk[:, c, :], qk_ps[:, c * W:(c + 1) * W], ACT.Relu,
                                             bias=bqk_sb[:, c:c + 1]).then_inc(act_qk, 1)
                        nc.scalar.activation(exp_qk[:, c, :], qk_ps[:, c * W:(c + 1) * W], ACT.Exp,
                                             bias=bqk_sb[:, c:c + 1]).then_inc(act_qk, 1)
                if third:
                    act.wait_ge(ls_ready, 2 * i - 2)
                    nc.scalar.activation(es[:], ls[:], ACT.Exp).then_inc(es_ready, 1)
                if second:
                    rstd(mv2, ln2, rs2, mv2_ready, ln2_ready, rs2_ready, i - 1)

            skewed(act, step)

            act.wait_ge(tab_ready, 1)
            with act.Fori(E // 2, E) as e:
                row = act.value_load(padrow[0:1, bass.ds(e, 1)], min_val=0, max_val=DUMMY)
                act.dma_start(xs_dram[bass.ds(row, P), :], pad_rows[:]).then_inc(pads_out_act, 16)

            def evac_xT(j, r):
                act.wait_ge(xT_made, j + 1)
                if not isinstance(j, int) or j >= R:
                    act.wait_ge(gu_made, j - (R - 1))
                nc.scalar.activation(xT[:, r % R, :], xT_ps[r % 2], ACT.Copy).then_inc(xT_ready, 1)

            def silu(j, r):
                act.wait_ge(gu_made, j + 1)
                if not isinstance(j, int) or j >= 2:
                    act.wait_ge(hh_ready, j - 1)
                nc.scalar.activation(sg[:, r % 2, :], gu_ps[r % 2][:, 0:FF], ACT.Silu).then_inc(sg_ready, 1)

            evac_xT(0, 0)
            with act.Fori(0, TILES // R - 1) as t:
                for r in range(R):
                    evac_xT_j = t * R + (r + 1)
                    act.wait_ge(xT_made, evac_xT_j + 1)
                    nc.scalar.activation(xT[:, (r + 1) % R, :], xT_ps[(r + 1) % 2], ACT.Copy).then_inc(xT_ready, 1)
                    act.wait_ge(gu_made, t * R + (r + 1))
                    nc.scalar.activation(sg[:, r % 2, :], gu_ps[r % 2][:, 0:FF], ACT.Silu).then_inc(sg_ready, 1)
            for j in range(TILES - R, TILES):
                if j + 1 < TILES:
                    evac_xT(j + 1, j + 1)
                silu(j, j)

            out_t = out.rearrange("(t p) d -> p t d", p=P)
            with act.Fori(0, SEQS // CB // 2) as t:
                for b in range(2):
                    act.wait_ge(sum_ready, t * 2 + (b + 1))
                    act.dma_start(out_t[:, bass.ds(t * 2 * CB + b * CB, CB), :],
                                  yb[:, b, :].rearrange("p (c d) -> p c d", d=D)).then_inc(stored[b], 16)

        @block.vector
        def _(dve):
            V = nc.vector
            n = [0]

            def link(ins):
                n[0] += 1
                ins.then_inc(dve_const, 1)
                dve.wait_ge(dve_const, n[0])

            V.memset(eps_ln[:], LN_EPS)
            V.memset(veo[:], 0.0)
            V.memset(cum[:, 1, :], 0.0)
            V.memset(onesf[:], 1.0)
            V.memset(decq[:, 0:1], 1.0)
            V.memset(bias_bf[:], 0.0)
            link(V.memset(eps_den[:], DEN_EPS))
            dve.wait_ge(act_const, 1)
            link(V.tensor_scalar_add(lam[:, 0:1], lam[:, 0:1], 1.0))
            link(V.reciprocal(lam[:, 1:2], lam[:, 0:1]))
            link(V.tensor_scalar(lam[:, 0:1], lam[:, 1:2], 0.01, 0.99, ALU.mult, ALU.add))
            for c in range(7):
                m = 1 << c
                link(V.tensor_scalar(decq[:, m:2 * m], decq[:, 0:m], lam[:, c % 2:c % 2 + 1], None, ALU.mult))
                link(V.tensor_tensor(lam[:, (c + 1) % 2:(c + 1) % 2 + 1], lam[:, c % 2:c % 2 + 1],
                                     lam[:, c % 2:c % 2 + 1], ALU.mult))
            link(V.reciprocal(deck[:], decq[:]))
            dve.wait_ge(pool_const, CONST_POOL)
            link(V.tensor_scalar(par_i[:], par_i[:], 4, 1, ALU.logical_shift_right, ALU.bitwise_and))
            link(V.tensor_copy(par[:, 1:2], par_i[:]))
            link(V.tensor_scalar(par[:, 0:1], par[:, 1:2], -1.0, 1.0, ALU.mult, ALU.add))
            scale = 1.0 / float(HD) ** 0.5
            link(V.tensor_scalar(dec_even[:], decq[:], par[:, 0:1], scale, ALU.mult, ALU.mult))
            link(V.tensor_scalar(dec_odd[:], decq[:], par[:, 1:2], scale, ALU.mult, ALU.mult))
            link(V.tensor_scalar_mul(embb[:], rows_sb[:, ROW_TOKB:ROW_TOKB + D], EMB_SCALE))

            dve.wait_ge(ebias_in, 48)
            q = slice(0, 96)
            link(V.tensor_copy(ebm[q, :], eb3[q, :]))
            V.tensor_copy(bias_bf[0:32, :], ebm[0:32, :])
            link(V.tensor_tensor(ebr[q, :], eb3[q, :], ebm[q, :], ALU.subtract))
            link(V.tensor_copy(ebm[q, :], ebr[q, :]))
            V.tensor_copy(bias_bf[32:64, :], ebm[32:64, :])
            link(V.tensor_tensor(ebr[q, :], ebr[q, :], ebm[q, :], ALU.subtract))
            V.tensor_copy(bias_bf[64:96, :], ebr[64:96, :])
            V.tensor_copy(sel[:], selp[:, :, None].broadcast_to([P, E, P])).then_inc(bias_ready, 1)

            lnb = rows_sb[:, None, ROW_LNB:ROW_LNB + D].broadcast_to([P, U, D])
            bout = rows_sb[:, None, ROW_BOUT:ROW_BOUT + D].broadcast_to([P, U, D])
            bgate = rows_sb[:, None, ROW_BGATE:ROW_BGATE + E].broadcast_to([P, U, E])

            def stats(src, st, mv, st_ready, mv_ready, u):
                for s in range(U):
                    ins = V.bn_stats(st[:, s, :], src(s))
                ins.then_inc(st_ready, 1)
                stands_first(dve, bias_ready)
                dve.wait_ge(st_ready, u)
                for s in range(U):
                    ins = V.bn_aggr(mv[:, s, :], st[:, s, :])
                ins.then_inc(mv_ready, 1)

            def later(i, k):
                return not isinstance(i, int) or i >= k

            def step(i, b, first, second, third):
                c = 1 - b
                if third:
                    dve.wait_ge(h2_ready, i - 1)
                    stats(lambda s: h2[:, bass.ds(i * U + (s - 2 * U), 1), :].rearrange("p a d -> p (a d)"), st3, mv3, st3_ready, mv3_ready, i - 1)
                if first:
                    for s in range(U):
                        if b == 0:
                            dve.wait_ge(emb_in[b][s], 8 * i + 16)
                        else:
                            dve.wait_ge(emb_in[b][s], 8 * i + 8)
                    V.scalar_tensor_tensor(out=h[:, b, :, :], in0=emb[:, b, :, :], scalar=EMB_SCALE,
                                           in1=embb[:, None, :].broadcast_to([P, U, D]), op0=ALU.mult,
                                           op1=ALU.add).then_inc(h_ready, 1)
                    dve.wait_ge(h_ready, i + 1)
                    stats(lambda s: h[:, b, s, :], st1, mv1, st1_ready, mv1_ready, i + 1)
                if second:
                    for g in range(2):
                        mask(g, i - 1)
                if first:
                    dve.wait_ge(rs1_ready, i + 1)
                    if later(i, 1):
                        dve.wait_ge(xnT_made, i)
                    for s in range(U):
                        V.tensor_scalar(xn[:, s, :], h[:, b, s, :], mv1[:, s, 0:1], rs1[:, s:s + 1],
                                        ALU.subtract, ALU.mult).then_inc(xn_ready, 1)
                if third:
                    dve.wait_ge(rs3_ready, i - 1)
                    if later(i, 4):
                        for q in range(TOP * U):
                            if b == 0:
                                dve.wait_ge(rows_out[b][q], 8 * i - 16)
                            else:
                                dve.wait_ge(rows_out[b][q], 8 * i - 24)
                    for s in range(U):
                        V.tensor_scalar(rr[:, b, 0, s, 0:D],
                                        h2[:, bass.ds(i * U + (s - 2 * U), 1), :].rearrange("p a d -> p (a d)"),
                                        mv3[:, s, 0:1], rs3[:, s:s + 1], ALU.subtract, ALU.mult).then_inc(rr0_ready, 1)
                if second:
                    for g in range(2, 4):
                        mask(g, i - 1)
                if third:
                    dve.wait_ge(lg_made, i - 1)
                    V.tensor_tensor(lg[:], lg_ps.rearrange("p (s e) -> p s e", e=E), bgate, ALU.add).then_inc(lg_ready, 1)
                    stands_first(dve, bias_ready)
                    dve.wait_ge(lg_ready, i - 1)
                    for s in range(U):
                        V.max(mx[:, s, :], lg[:, s, :]).then_inc(mx_ready, 1)
                    dve.wait_ge(mx_ready, 2 * i - 2)
                    m1 = mx[:, :, 0:1]
                    V.tensor_tensor(ls[:, :, 0:E], lg[:], m1.broadcast_to([P, U, E]), ALU.subtract).then_inc(ls_ready, 1)
                    V.tensor_tensor(ls[:, :, E:E + TOP], mx[:, :, 0:TOP], m1.broadcast_to([P, U, TOP]),
                                    ALU.subtract).then_inc(ls_ready, 1)
                    for s in range(U):
                        V.max_index(mi[:, s, :], mx[:, s, :], lg[:, s, :]).then_inc(mi_ready, 1)
                    dve.wait_ge(mi_ready, 2 * i - 2)
                    V.tensor_copy(mif[:], mi[:, :, 0:TOP]).then_inc(mif_ready, 1)
                if second:
                    dve.wait_ge(den_ready, i)
                    V.reciprocal(rec[:], den_sb[:]).then_inc(rec_ready, 1)
                    dve.wait_ge(rec_ready, i)
                    V.tensor_tensor(oT[:], num_ps, rec[:], ALU.mult).then_inc(oT_ready, 1)
                    V.tensor_tensor(hlb[:], h[:, c, :, :], lnb, ALU.add)
                if third:
                    dve.wait_ge(mif_ready, i - 1)
                    for k in range(TOP):
                        V.tensor_tensor(mk[:, k, :, :], iota_e[:, None, :].broadcast_to([P, U, E]),
                                        mif[:, :, k:k + 1].broadcast_to([P, U, E]), ALU.is_equal).then_inc(mk_ready, 1)
                    dve.wait_ge(mk_ready, 2 * i - 2)
                    V.tensor_tensor(msum[:], mk[:, 0, :, :], mk[:, 1, :, :], ALU.add).then_inc(msum_ready, 1)
                if first:
                    dve.wait_ge(act_qk, 4 * i + 4)
                    V.scalar_tensor_tensor(out=qk[:], in0=exp_qk[:], scalar=1.0, in1=relu_qk[:],
                                           op0=ALU.min, op1=ALU.add).then_inc(qk_ready, 1)
                    dve.wait_ge(qk_ready, i + 1)
                    q2 = qk[:, 0, :].rearrange("p (s l) -> p s l", l=P)
                    V.tensor_tensor(kd[:, b, :].rearrange("p (s l) -> p s l", l=P),
                                    qk[:, 1, :].rearrange("p (s l) -> p s l", l=P),
                                    deck[:, None, :].broadcast_to([P, U, P]), ALU.mult).then_inc(kq_ready, 1)
                    V.tensor_tensor(qeo[:, b, :, 0, :], q2, dec_even[:, None, :].broadcast_to([P, U, P]),
                                    ALU.mult).then_inc(kq_ready, 1)
                    V.tensor_tensor(qeo[:, b, :, 1, :], q2, dec_odd[:, None, :].broadcast_to([P, U, P]),
                                    ALU.mult).then_inc(kq_ready, 1)
                    dve.wait_ge(v_made, i + 1)
                    for q in range(2):
                        cols = slice(None)
                        V.tensor_tensor(
                            veo[:, b, :, q, :].rearrange("p s (g q f) -> p s g q f", q=2, f=HD)[:, :, :, q, :],
                            v_ps.rearrange("p (s g q f) -> p s g q f", s=U, q=2, f=HD)[:, :, :, q, :],
                            rows_sb[:, None, ROW_BV:ROW_BV + D].broadcast_to([P, U, D])
                            .rearrange("p s (g q f) -> p s g q f", q=2, f=HD)[:, :, :, q, :],
                            ALU.add).then_inc(v_ready, 1)
                if second:
                    dve.wait_ge(ao_made, i)
                    V.tensor_tensor(ao[:], ao_ps.rearrange("p (s d) -> p s d", d=D), bout, ALU.add).then_inc(ao_ready, 1)
                    dve.wait_ge(ao_ready, i)
                    stats(lambda s: ao[:, s, :], st2, mv2, st2_ready, mv2_ready, i)
                if third:
                    dve.wait_ge(es_ready, i - 1)
                    V.tensor_reduce(ssum[:], es[:, :, 0:E], AXX, ALU.add).then_inc(ssum_ready, 1)
                    dve.wait_ge(ssum_ready, i - 1)
                    V.reciprocal(rsum[:], ssum[:]).then_inc(rsum_ready, 1)
                    V.tensor_copy(rr[:, b, :, :, D + 1].bitcast(I32), tokid[:, :, bass.ds(i * U - 2 * U, U)])
                    dve.wait_ge(rsum_ready, i - 1)
                    V.tensor_tensor(rr[:, b, :, :, D].rearrange("p k s -> p s k"), es[:, :, E:E + TOP],
                                    rsum[:, :, None].broadcast_to([P, U, TOP]), ALU.mult).then_inc(w_ready[b], 1)
                if second:
                    dve.wait_ge(mv2_ready, i)
                    for s in range(U):
                        V.scalar_tensor_tensor(out=aog[:, s, :], in0=ao[:, s, :], scalar=mv2[:, s, 0:1],
                                               in1=rows_sb[:, ROW_LNG:ROW_LNG + D], op0=ALU.subtract,
                                               op1=ALU.mult).then_inc(aog_ready, 1)
                    dve.wait_ge(rs2_ready, i)
                    dve.wait_ge(aog_ready, 2 * i)
                    for s in range(U):
                        ins = V.scalar_tensor_tensor(
                            out=h2[:, bass.ds(i * U + (s - U), 1), :].rearrange("p a d -> p (a d)"), in0=aog[:, s, :],
                            scalar=rs2[:, s:s + 1], in1=hlb[:, s, :], op0=ALU.mult, op1=ALU.add)
                    ins.then_inc(h2_ready, 1)
                if third:
                    dve.wait_ge(rk_made, i - 1)
                    V.tensor_tensor(rank[:], rk_ps.rearrange("p (s e) -> p s e", e=E),
                                    eoff[:, None, :].broadcast_to([P, U, E]), ALU.add).then_inc(rank_ready, 1)
                    V.tensor_tensor(mpair[:], msum[:, 0, :], msum[:, 1, :], ALU.add).then_inc(mpair_ready, 1)
                    dve.wait_ge(rank_ready, i - 1)
                    for k in range(TOP):
                        V.tensor_tensor(slotp[:, k, :, :], rank[:], mk[:, k, :, :], ALU.mult).then_inc(slotp_ready, 1)
                    dve.wait_ge(mpair_ready, i - 1)
                    V.tensor_tensor(cum[:, b, :], cum[:, c, :], mpair[:], ALU.add).then_inc(cum_ready, 1)
                    dve.wait_ge(slotp_ready, 2 * i - 2)
                    V.tensor_reduce(slotf[:], slotp[:], AXX, ALU.add).then_inc(slotf_ready, 1)
                    dve.wait_ge(slotf_ready, i - 1)
                    V.tensor_copy(slot[:, b, :, :], slotf[:]).then_inc(slot_ready[b], 1)

            def mask(g, u):
                dve.wait_ge(sc_made, u * 4 + (g + 1))
                if later(u, 1):
                    dve.wait_ge(nd_made, u)
                V.tensor_tensor(sm[:, g, :, :], sc_ps[g][:].rearrange("p (a l) -> p a l", l=P),
                                causal[:, None, :].broadcast_to([P, 2 * U, P]), ALU.mult).then_inc(sm_ready, 1)

            skewed(dve, step)

            k = [0]

            def tstep(ins):
                k[0] += 1
                ins.then_inc(tab_step, 1)
                dve.wait_ge(tab_step, k[0])

            dve.wait_ge(cnt_made, 1)
            tstep(V.tensor_copy(cnt[:], cnt_ps))
            tstep(V.tensor_tensor(padrow_f[:], cnt[:], eoff[:], ALU.add))
            V.tensor_copy(padrow[:], padrow_f[:]).then_inc(tab_ready, 1)
            tstep(V.tensor_scalar_add(cnt[:], cnt[:], float(P - 1)))
            tstep(V.tensor_copy(cnt_i[:], cnt[:]))
            tstep(V.tensor_scalar(nt_i[:], cnt_i[:], 7, None, ALU.logical_shift_right))
            tstep(V.tensor_copy(ntf[:], nt_i[:]))
            tstep(V.tensor_tensor_scan(endt[:], onesf[:], ntf[:], 0.0, ALU.mult, ALU.add))
            tstep(V.tensor_scalar(passed[:], endt[:], tileno[:, 0:1], None, ALU.is_le))
            tstep(V.tensor_tensor(passn[:], passed[:], ntf[:], ALU.mult))
            tstep(V.tensor_reduce(tab[:, 0:1], passed[:], AXX, ALU.add))
            tstep(V.tensor_reduce(tab[:, 1:2], passn[:], AXX, ALU.add))
            tstep(V.tensor_tensor(tab[:, 1:2], tileno[:], tab[:, 1:2], ALU.subtract))
            tstep(V.tensor_scalar_mul(tab[:, 2:3], tab[:, 0:1], float(REG)))
            tstep(V.tensor_scalar_mul(tab[:, 1:2], tab[:, 1:2], float(P)))
            tstep(V.tensor_tensor(tab[:, 1:2], tab[:, 1:2], tab[:, 2:3], ALU.add))
            tstep(V.tensor_scalar_min(tab[:, 1:2], tab[:, 1:2], float(DUMMY)))
            tstep(V.tensor_scalar_min(tab[:, 0:1], tab[:, 0:1], float(E - 1)))
            dve.wait_ge(tab_made, 1)
            V.tensor_copy(tab_e[:], tab_ps[0:1, 0:TILES]).then_inc(tab_ready, 1)
            V.tensor_copy(tab_b[:], tab_ps[0:1, P:P + TILES]).then_inc(tab_ready, 1)

            def copy_widx(t, r):
                j = t * R + r
                dve.wait_ge(xs_in[r % R], lap(t, r) * 16)
                if later(j, R):
                    dve.wait_ge(y_out[r % R], lap(t, r) * 16 - 16)
                V.tensor_copy(widx[:, r % R, :], xs[:, r % R, D:D + 2]).then_inc(widx_ready, 1)

            def gate(t, r):
                j = t * R + r
                dve.wait_ge(sg_ready, j + 1)
                if later(j, 2):
                    dve.wait_ge(hT_made, j - 1)
                V.tensor_tensor(hh[:, r % 2, :], gu_ps[r % 2][:, FF:2 * FF], sg[:, r % 2, :], ALU.mult).then_inc(hh_ready, 1)

            def evac_hT(t, r):
                j = t * R + r
                dve.wait_ge(hT_made, j + 1)
                if later(j, 2):
                    dve.wait_ge(y_made, j - 1)
                V.tensor_copy(hT[:, r % 2, :], hT_ps[r % 2]).then_inc(hT_ready, 1)

            def evac_y(t, r):
                j = t * R + r
                dve.wait_ge(y_made, j + 1)
                V.tensor_scalar(ysb[:, r % R, :], y_ps[r % 2], widx[:, r % R, 0:1], None, ALU.mult).then_inc(y_ready[r % R], 1)

            def estep(t, r, full):
                if full or r + 1 < TILES:
                    copy_widx(t, r + 1)
                if full or r < TILES:
                    gate(t, r)
                if full or 0 <= r - 1 < TILES:
                    evac_hT(t, r - 1)
                if full or 0 <= r - 2 < TILES:
                    evac_y(t, r - 2)

            copy_widx(0, 0)
            for j in range(R):
                estep(0, j, False)
            with dve.Fori(1, TILES // R - 1) as t:
                for r in range(R):
                    estep(t, r, True)
            for j in range(TILES - R, TILES + 2):
                estep(0, j, False)

            with dve.Fori(0, SEQS // CB // 2) as t:
                for b in range(2):
                    dve.wait_ge(ya_in[b], t * 16 + 16)
                    dve.wait_ge(yb_in[b], t * 16 + 16)
                    V.tensor_tensor(ya[:, b, :], ya[:, b, :], yb[:, b, :], ALU.add).then_inc(sum1_ready, 1)
                    dve.wait_ge(sum1_ready, t * 2 + (b + 1))
                    V.tensor_tensor(yb[:, b, :].rearrange("p (c d) -> p c d", d=D), ya[:, b, :].rearrange("p (c d) -> p c d", d=D),
                                    h2[:, bass.ds(t * 2 * CB + b * CB, CB), :], ALU.add).then_inc(sum_ready, 1)

        @block.tensor
        def _(pe):
            M = nc.tensor.matmul

            def later(i, k):
                return not isinstance(i, int) or i >= k

            pe.wait_ge(small_in, 16 * 6)
            pe.wait_ge(pool_const, CONST_POOL)

            def step(i, b, first, second, third):
                c = 1 - b
                if second:
                    pe.wait_ge(kq_ready, 3 * i)
                    if later(i, 2):
                        pe.wait_ge(sm_ready, 4 * i - 4)
                    for s in range(U):
                        for g in range(4):
                            rows_g = slice(32 * g, 32 * g + 32)
                            ins = M(sc_ps[g][:, s * 2 * P:(s + 1) * 2 * P], kd[rows_g, c, s * P:(s + 1) * P],
                                    qeo[rows_g, c, s, :, :].rearrange("p q l -> p (q l)"), start=True, stop=True)
                            if s == U - 1:
                                ins.then_inc(sc_made, 1)
                if first:
                    pe.wait_ge(xn_ready, 2 * i + 2)
                    if later(i, 1):
                        pe.wait_ge(v_ready, 2 * i)
                    for s in range(U):
                        ins = nc.tensor.transpose(xnT_ps[:, s * P:(s + 1) * P], xn[:, s, :], ident[:])
                    ins.then_inc(xnT_made, 1)
                if third:
                    pe.wait_ge(rr0_ready, 2 * i - 2)
                    if later(i, 3):
                        pe.wait_ge(rank_ready, i - 2)
                    for s in range(U):
                        ins = nc.tensor.transpose(x2T_ps[:, s * P:(s + 1) * P], rr[:, b, 0, s, 0:D], ident[:])
                    ins.then_inc(x2T_made, 1)
                if second:
                    pe.wait_ge(sm_ready, 4 * i)
                    pe.wait_ge(v_ready, 2 * i)
                    if later(i, 2):
                        pe.wait_ge(ao_ready, i - 1)
                    for s in range(U):
                        for q in range(2):
                            for g in range(4):
                                M(num_ps[32 * g:32 * g + 32, s * P:(s + 1) * P], veo[:, c, s, q, 32 * g:32 * g + 32],
                                  sm[:, g, 2 * s + q, :], start=(q == 0), stop=(q == 1))
                    for s in range(U):
                        for q in range(2):
                            for g in range(4):
                                ins = M(den_ps[32 * g:32 * g + 32, s * P:(s + 1) * P], den_w[:, q, :],
                                        sm[:, g, 2 * s + q, :], start=(q == 0), stop=(q == 1))
                    ins.then_inc(nd_made, 1)
                if first:
                    pe.wait_ge(xnT_ready, i + 1)
                    if later(i, 1):
                        pe.wait_ge(act_qk, 4 * i)
                    M(qk_ps[:, 0:W], wqkv_sb[:, 0:D], xnT[:], start=True, stop=True)
                    M(qk_ps[:, W:2 * W], wqkv_sb[:, D:2 * D], xnT[:], start=True, stop=True).then_inc(qk_made, 1)
                    for s in range(U):
                        ins = M(v_ps[:, s * D:(s + 1) * D], xnT[:, s * P:(s + 1) * P], wqkv_sb[:, 2 * D:3 * D],
                                start=True, stop=True)
                    ins.then_inc(v_made, 1)
                if third:
                    pe.wait_ge(x2T_ready, i - 1)
                    for s in range(U):
                        ins = M(lg_ps[:, s * E:(s + 1) * E], x2T[:, s * P:(s + 1) * P], wgate_sb[:], start=True, stop=True)
                    ins.then_inc(lg_made, 1)
                if second:
                    pe.wait_ge(oT_ready, i)
                    for s in range(U):
                        ins = M(ao_ps[:, s * D:(s + 1) * D], oT[:, s * P:(s + 1) * P], wout_sb[:], start=True, stop=True)
                    ins.then_inc(ao_made, 1)
                if third:
                    pe.wait_ge(msum_ready, i - 1)
                    pe.wait_ge(lg_ready, i - 1)
                    if later(i, 3):
                        pe.wait_ge(cum_ready, i - 2)
                    M(rk_ps, tri[:], msum[:].rearrange("p s e -> p (s e)"), start=True, stop=False)
                    M(rk_ps.rearrange("p (s e) -> p s e", e=E), ones_bf[:], cum[:, c:c + 1, :].broadcast_to([P, U, E]), start=False, stop=False)
                    M(rk_ps[:, E:2 * E], ones_bf[:], msum[:, 0, :], start=False, stop=True).then_inc(rk_made, 1)

            skewed(pe, step)

            pe.wait_ge(cum_ready, UNITS)
            pe.wait_ge(rank_ready, UNITS)
            M(cnt_ps, ones_bf[:], cum[:, (UNITS + 1) % 2, :], start=True, stop=True).then_inc(cnt_made, 1)
            pe.wait_ge(tab_step, 17)
            for q in range(2):
                ins = M(tab_ps[0:1, q * P:(q + 1) * P], tab[:, q:q + 1], ident[:], start=True, stop=True)
            ins.then_inc(tab_made, 1)
            pe.wait_ge(tab_ready, 3)
            pe.wait_ge(experts_in, 16 * 12)
            pe.wait_ge(bias_ready, 1)

            def trans_x(t, r):
                j = t * R + r
                pe.wait_ge(xs_in[r % R], lap(t, r) * 16)
                if later(j, 2):
                    pe.wait_ge(xT_ready, j - 1)
                nc.tensor.transpose(xT_ps[r % 2], xs[:, r % R, 0:D], ident[:]).then_inc(xT_made, 1)

            def gate_up(t, r):
                j = t * R + r
                e = pe.value_load(tab_e[0:1, bass.ds(j, 1)], min_val=0, max_val=E - 1)
                pe.wait_ge(xT_ready, j + 1)
                if later(j, 2):
                    pe.wait_ge(hh_ready, j - 1)
                M(gu_ps[r % 2][:], xT[:, r % R, :], wgu_sb[:, bass.ds(e * (2 * FF), 2 * FF)], start=True, stop=False)
                M(gu_ps[r % 2][:], sel[:, bass.ds(e, 1), :].rearrange("p a t -> p (a t)"), bias_bf[:, 0:2 * FF],
                  start=False, stop=True).then_inc(gu_made, 1)

            def trans_h(t, r):
                j = t * R + r
                pe.wait_ge(hh_ready, j + 1)
                if later(j, 2):
                    pe.wait_ge(hT_ready, j - 1)
                for q in range(2):
                    ins = nc.tensor.transpose(hT_ps[r % 2][:, q * P:(q + 1) * P], hh[:, r % 2, q * P:(q + 1) * P], ident[:])
                ins.then_inc(hT_made, 1)

            def down(t, r):
                j = t * R + r
                e = pe.value_load(tab_e[0:1, bass.ds(j, 1)], min_val=0, max_val=E - 1)
                pe.wait_ge(hT_ready, j + 1)
                if later(j, 2):
                    pe.wait_ge(y_ready[(r - 2) % R], lap(t, r - 2))
                for q in range(2):
                    M(y_ps[r % 2], hT[:, r % 2, q * P:(q + 1) * P], wd_sb[:, bass.ds(e * (2 * D) + q * D, D)],
                      start=(q == 0), stop=False)
                M(y_ps[r % 2], sel[:, bass.ds(e, 1), :].rearrange("p a t -> p (a t)"), bias_bf[:, 2 * FF:BIAS_N],
                  start=False, stop=True).then_inc(y_made, 1)

            def estep(t, r, full):
                if full or r + 1 < TILES:
                    trans_x(t, r + 1)
                if full or r < TILES:
                    gate_up(t, r)
                if full or 0 <= r - 1 < TILES:
                    trans_h(t, r - 1)
                if full or 0 <= r - 2 < TILES:
                    down(t, r - 2)

            trans_x(0, 0)
            for j in range(R):
                estep(0, j, False)
            with pe.Fori(1, TILES // R - 1) as t:
                for r in range(R):
                    estep(t, r, True)
            for j in range(TILES - R, TILES + 2):
                estep(0, j, False)


def kernel(**inputs):
    import numpy as np
    import concourse.bacc as bacc
    from concourse.bass_utils import run_bass_kernel_spmd

    a = {k: np.ascontiguousarray(v) for k, v in inputs.items()}
    b_qkv = a["L0_attn_b_qkv"]
    arrays = {
        "ids": np.ascontiguousarray(a["x"].T).view(np.uint32),
        "wt": np.ascontiguousarray(a["L0_tok_W"].T),
        "rows": np.concatenate([a["L0_tok_b"], b_qkv[2 * D:], a["L0_attn_b_out"], a["L0_attn_ln_g"],
                                a["L0_attn_ln_b"], a["L0_ffn_bgate"]]),
        "bqk": np.ascontiguousarray(b_qkv[:2 * D].reshape(2, D).T),
        "decay": np.ascontiguousarray(np.broadcast_to(a["L0_attn_decay_logits"][:, None], (HEADS, HD)).reshape(D, 1)),
        "wqkv": a["L0_attn_W_qkv"],
        "wout": a["L0_attn_W_out"],
        "wgate": a["L0_ffn_Wgate"],
        "wgu": np.ascontiguousarray(np.concatenate([a["L0_ffn_Wg"], a["L0_ffn_Wu"]], axis=2).transpose(1, 0, 2)
                                    .reshape(P, E * 2 * FF)),
        "wd": np.ascontiguousarray(a["L0_ffn_Wd"].reshape(E, 2, P, D).transpose(2, 0, 1, 3).reshape(P, E * 2 * D)),
        "ebias": np.concatenate([a["L0_ffn_bg"], a["L0_ffn_bu"], a["L0_ffn_bd"]], axis=1),
    }
    nc = bacc.Bacc("TRN2", target_bir_lowering=False, num_devices=1)
    args = [nc.dram_tensor(k, v.shape, mybir.dt.from_np(v.dtype), kind="ExternalInput").ap() for k, v in arrays.items()]
    args.append(nc.dram_tensor("out", (TOK, D), F32, kind="ExternalOutput").ap())
    build(nc, *args)
    r = run_bass_kernel_spmd(nc, [arrays], core_ids=[0])
    return r.results[0]["out"].reshape(SEQS, P, D)
```

```python
from contextlib import ExitStack

import concourse.bass as bass
from concourse import mybir

F32 = mybir.dt.float32
BF16 = mybir.dt.bfloat16
I32 = mybir.dt.int32
U32 = mybir.dt.uint32
ALU = mybir.AluOpType
ACT = mybir.ActivationFunctionType
AXX = mybir.AxisListType.X
NOT_EQUAL = ALU.not_equal

P = 128
SEQS = 32
D = 128
HEADS = 8
HD = D // HEADS
E = 32
FF = 256
TOP = 2
TOK = SEQS * P
U = 2
UNITS = SEQS // U
W = U * P
REG = TOK + P
TILES = TOP * TOK // P + E
ROW = D + 2
DUMMY = E * REG
SKIP = 1 << 20
LN_EPS = 1e-5
DEN_EPS = 1e-6
EMB_SCALE = float(D) ** 0.5
ROW_TOKB, ROW_BV, ROW_BOUT, ROW_LNG, ROW_LNB, ROW_BGATE = (D * i for i in range(6))
ROWS_N = 5 * D + E
PADS = 16
BIAS_N = 2 * FF + D


def build(nc, ids, wt, rows, bqk, decay, wqkv, wout, wgate, wgu, wd, ebias, out):
    ctx = ExitStack()
    with ctx:
        def sb(name, shape, dt=F32):
            return ctx.enter_context(nc.sbuf_tensor(name, shape, dt))

        def ps(name, shape, dt=F32):
            return ctx.enter_context(nc.psum_tensor(name, shape, dt))

        def sem(name):
            return ctx.enter_context(nc.semaphore(name))

        xs_dram = nc.dram_tensor("dispatched_rows", [E * REG + P, ROW], F32, kind="Internal").ap()
        y_dram = nc.dram_tensor("expert_rows", [TOP * TOK, D], F32, kind="Internal").ap()

        wgu_sb = sb("wgu_sb", [P, E * 2 * FF])
        wd_sb = sb("wd_sb", [P, E * 2 * D])
        wqkv_sb = sb("wqkv_sb", [P, 3 * D])
        wout_sb = sb("wout_sb", [P, D])
        wgate_sb = sb("wgate_sb", [P, E])
        rows_sb = sb("rows_sb", [P, ROWS_N])
        bqk_sb = sb("bqk_sb", [P, 2])
        dl_sb = sb("dl_sb", [P, 1])
        lam = sb("lam", [P, 2])
        ids_sb = sb("ids_sb", [P, SEQS], U32)
        ids_now = sb("ids_now", [P, 2, U], U32)
        decq = sb("decq", [P, P])
        decqm = sb("decqm", [P, 2, P])
        deck = sb("deck", [P, P])
        causal = sb("causal", [P, P])
        ident = sb("ident", [P, P])
        tri = sb("tri", [P, P], BF16)
        ones_bf = sb("ones_bf", [P, P], BF16)
        par_i = sb("par_i", [P, 1], I32)
        rowno = sb("rowno", [P, 1], I32)
        par = sb("par", [P, 2])
        iota_e = sb("iota_e", [P, E])
        eoff = sb("eoff", [P, E])
        tokid = sb("tokid", [P, TOP, SEQS], I32)
        pad_rows = sb("pad_rows", [P, PADS, ROW])
        bias_bf = sb("bias_bf", [P, BIAS_N + 2 * D], BF16)
        selp = sb("selp", [P, E], BF16)
        sel = sb("sel", [P, E, P], BF16)
        eps_ln = sb("eps_ln", [P, 1])
        h2 = sb("h2", [P, SEQS, D])

        emb = sb("emb", [P, 2, U, D])
        h = sb("h", [P, 2, U, D])
        nm1 = sb("nm1", [P, U])
        nm2 = sb("nm2", [P, U])
        nm3 = sb("nm3", [P, U])
        st1 = sb("st1", [P, U, 6])
        mv1 = sb("mv1", [P, U, 2])
        ln1 = sb("ln1", [P, U])
        rs1 = sb("rs1", [P, U])
        xn = sb("xn", [P, U, D])
        xnT = sb("xnT", [P, W])
        relu_qk = sb("relu_qk", [P, 2, W])
        exp_qk = sb("exp_qk", [P, 2, W])
        qk = sb("qk", [P, 2, W])
        kd = sb("kd", [P, 2, W])
        qz = sb("qz", [P, U, 4, 2, P])
        qd = sb("qd", [P, W])
        vx = sb("vx", [P, 2, U, HEADS, HD + 1])
        sm = sb("sm", [P, 4, U * 2, P])
        eb3 = sm[:, 0:2, :, :].rearrange("p b c d -> p (b c d)")[:, 0:BIAS_N + 2 * D]
        ebm = sm[:, 2:4, :, :].rearrange("p b c d -> p (b c d)")[:, 0:(BIAS_N + 2 * D) // 2].bitcast(BF16)
        den = sb("den", [P, U * HEADS])
        rec = sb("rec", [P, U * HEADS])
        o = sb("o", [P, U, D])
        oT = sb("oT", [P, W])
        aon = sb("aon", [P, U, D])
        hlb = sb("hlb", [P, U, D])
        st2 = sb("st2", [P, U, 6])
        mv2 = sb("mv2", [P, U, 2])
        ln2 = sb("ln2", [P, U])
        rs2 = sb("rs2", [P, U])
        aog = sb("aog", [P, U, D])
        st3 = sb("st3", [P, U, 6])
        mv3 = sb("mv3", [P, U, 2])
        ln3 = sb("ln3", [P, U])
        rs3 = sb("rs3", [P, U])
        rr = sb("rr", [P, 2, TOP, U, ROW])
        x2T = sb("x2T", [P, W])
        lg = sb("lg", [P, U, E])
        mx = sb("mx", [P, U, 8])
        mi = sb("mi", [P, U, 8], U32)
        mif = sb("mif", [P, U, TOP])
        ls = sb("ls", [P, U, E + TOP])
        es = sb("es", [P, U, E + TOP])
        ssum = sb("ssum", [P, U])
        rsum = sb("rsum", [P, U])
        mk = sb("mk", [P, TOP, U, E])
        msum = sb("msum", [P, U, E], BF16)
        cum = sb("cum", [P, 2, E], BF16)
        mpair = sb("mpair", [P, E], BF16)
        rank = sb("rank", [P, U, E])
        slotp = sb("slotp", [P, TOP, U, E])
        slotf = sb("slotf", [P, TOP, U])
        slot = sb("slot", [P, 2, TOP, U], U32)

        cnt = sb("cnt", [P, E])
        cnt_i = sb("cnt_i", [P, E], I32)
        nt_i = sb("nt_i", [P, E], I32)
        ntf = sb("ntf", [P, E])
        onesf = sb("onesf", [P, E])
        endt = sb("endt", [P, E])
        tileno = sb("tileno", [P, 1])
        passed = sb("passed", [P, E])
        passn = sb("passn", [P, E])
        tab = sb("tab", [P, 4])
        padrow_f = sb("padrow_f", [P, E])
        pad_e = sb("pad_e", [P, 1])
        pad_q = sb("pad_q", [P, 1])
        pad_i = sb("pad_i", [P, 2], I32)
        padsel = sb("padsel", [P, E])
        padq = sb("padq", [P, 4])
        padbase = sb("padbase", [P, 1])
        padidx = sb("padidx", [P, 4], U32)
        padblk = sb("padblk", [P, 1])
        padblk_i = sb("padblk_i", [P, 1], I32)
        padbidx = sb("padbidx", [P, 2], U32)
        tab_e = sb("tab_e", [1, TILES], I32)
        tab_b = sb("tab_b", [1, TILES], I32)

        R = 8
        xs = sb("xs", [P, R, ROW])
        widx = sb("widx", [P, R, 2])
        xT = sb("xT", [P, R, P])
        sg = sb("sg", [P, 2, FF])
        hh = sb("hh", [P, 2, FF])
        hT = sb("hT", [P, 2, FF])
        ysb = sb("ysb", [P, R, D])
        CB = 4
        ya = wgu_sb[:, 0:SEQS * D].rearrange("p (t d) -> p t d", d=D)
        yb = wgu_sb[:, SEQS * D:2 * SEQS * D].rearrange("p (t d) -> p t d", d=D)

        bank = [ps(f"bank{i}", [P, 512]) for i in range(8)]
        sc_ps = bank[0:4]
        xnT_ps = bank[4][:, 0:W]
        v_ps = bank[4][:, W:2 * W]
        qk_ps = bank[5]
        nd_ps = bank[6][:, 0:U * HEADS * (HD + 1)].rearrange("p (a f) -> p a f", f=HD + 1)
        oT_ps = bank[6][:, 0:W]
        ao_ps = bank[6][:, W:2 * W]
        x2T_ps = bank[7][:, 0:W]
        lg_ps = bank[7][:, W:W + U * E]
        rk_ps = bank[7][:, W + U * E:W + 2 * U * E]
        cnt_ps = bank[7][:, W + 2 * U * E:W + 2 * U * E + E]
        tab_ps = bank[5]
        gu_ps = [bank[0], bank[1]]
        hT_ps = [bank[2][:, 0:FF], bank[3][:, 0:FF]]
        xT_ps = [bank[4][:, 0:P], bank[5][:, 0:P]]
        y_ps = [bank[6][:, 0:D], bank[7][:, 0:D]]

        ids_in = sem("ids_in")
        small_in = sem("small_in")
        ebias_in = sem("ebias_in")
        experts_in = sem("experts_in")
        pool_const = sem("pool_const")
        dve_const = sem("dve_const")
        act_const = sem("act_const")
        bias_ready = sem("bias_ready")
        ids_staged_first = sem("ids_staged_first")
        ids_staged = [sem(f"ids_staged{b}") for b in range(2)]
        emb_in = [[sem(f"emb_in{b}{s}") for s in range(U)] for b in range(2)]
        emb_sum = sem("emb_sum")
        hlb_ready = sem("hlb_ready")
        h_ready = sem("h_ready")
        nm1_ready = sem("nm1_ready")
        nm2_ready = sem("nm2_ready")
        nm3_ready = sem("nm3_ready")
        kd_ready = sem("kd_ready")
        qd_ready = sem("qd_ready")
        qeo_ready = sem("qeo_ready")
        qz_ready = sem("qz_ready")
        den_ready = sem("den_ready")
        o_ready = sem("o_ready")
        oT_made = sem("oT_made")
        aon_ready = sem("aon_ready")
        st1_ready = sem("st1_ready")
        mv1_ready = sem("mv1_ready")
        ln1_ready = sem("ln1_ready")
        rs1_ready = sem("rs1_ready")
        xn_ready = sem("xn_ready")
        xnT_made = sem("xnT_made")
        xnT_ready = sem("xnT_ready")
        qk_made = sem("qk_made")
        v_made = sem("v_made")
        act_qk = sem("act_qk")
        qk_ready = sem("qk_ready")
        v_ready = sem("v_ready")
        sc_made = sem("sc_made")
        sm_ready = sem("sm_ready")
        nd_made = sem("nd_made")
        rec_ready = sem("rec_ready")
        oT_ready = sem("oT_ready")
        ao_made = sem("ao_made")
        st2_ready = sem("st2_ready")
        mv2_ready = sem("mv2_ready")
        ln2_ready = sem("ln2_ready")
        rs2_ready = sem("rs2_ready")
        aog_ready = sem("aog_ready")
        h2_ready = sem("h2_ready")
        st3_ready = sem("st3_ready")
        mv3_ready = sem("mv3_ready")
        ln3_ready = sem("ln3_ready")
        rs3_ready = sem("rs3_ready")
        rr0_ready = sem("rr0_ready")
        rr1_ready = [sem(f"rr1_ready{b}") for b in range(2)]
        x2T_made = sem("x2T_made")
        x2T_ready = sem("x2T_ready")
        lg_made = sem("lg_made")
        lg_ready = sem("lg_ready")
        mx_ready = sem("mx_ready")
        mi_ready = sem("mi_ready")
        mif_ready = sem("mif_ready")
        ls_ready = sem("ls_ready")
        es_ready = sem("es_ready")
        ssum_ready = sem("ssum_ready")
        rsum_ready = sem("rsum_ready")
        w_ready = [sem(f"w_ready{b}") for b in range(2)]
        mk_ready = sem("mk_ready")
        msum_ready = sem("msum_ready")
        mpair_ready = sem("mpair_ready")
        cum_ready = sem("cum_ready")
        rk_made = sem("rk_made")
        rank_ready = sem("rank_ready")
        slotp_ready = sem("slotp_ready")
        slotf_ready = sem("slotf_ready")
        slot_ready = [sem(f"slot_ready{b}") for b in range(2)]
        rows_out = [[sem(f"rows_out{b}{c}") for c in range(TOP * U)] for b in range(2)]
        cnt_made = sem("cnt_made")
        tab_step = sem("tab_step")
        tab_made = sem("tab_made")
        tab_ready = sem("tab_ready")
        pads_out = sem("pads_out")
        padidx_ready = sem("padidx_ready")
        xs_in = [sem(f"xs_in{r}") for r in range(R)]
        widx_ready = sem("widx_ready")
        xT_made = sem("xT_made")
        xT_ready = sem("xT_ready")
        gu_made = sem("gu_made")
        sg_ready = sem("sg_ready")
        hh_ready = sem("hh_ready")
        hT_made = sem("hT_made")
        hT_ready = sem("hT_ready")
        y_made = sem("y_made")
        y_ready = [sem(f"y_ready{r}") for r in range(R)]
        y_out = [sem(f"y_out{r}") for r in range(R)]
        ya_in = [sem(f"ya_in{c}") for c in range(SEQS // CB)]
        yb_in = [sem(f"yb_in{c}") for c in range(SEQS // CB)]
        sum1_ready = sem("sum1_ready")
        sum_ready = sem("sum_ready")
        stored = sem("stored")

        CONST_POOL = 20
        TAB_STEPS = 23

        block = ctx.enter_context(nc.Block())

        def lap(t, q):
            return t + (q // R + 1)

        def stands_first(eng, passed):
            eng.wait_ge(passed, 1)

        def steps(eng, step, first, last):
            n = (last - first) // 2
            if n > 1:
                with eng.Fori(0, n) as t:
                    for k in range(2):
                        step(t * 2 + (first + k), (first + k) % 2)
            else:
                n = 0
            for i in range(first + 2 * n, last):
                step(i, i % 2)

        def skewed(eng, step):
            step(-1, 1, True, False, False, False)
            step(0, 0, True, True, False, False)
            step(1, 1, True, True, True, False)
            step(2, 0, True, True, True, True)
            step(3, 1, True, True, True, True)
            steps(eng, lambda i, b: step(i, b, True, True, True, True), 4, UNITS - 1)
            step(UNITS - 1, (UNITS - 1) % 2, False, True, True, True)
            step(UNITS, UNITS % 2, False, False, True, True)
            step(UNITS + 1, (UNITS + 1) % 2, False, False, False, True)

        @block.sync
        def _(sp):
            sp.dma_start(ids_sb[:], ids).then_inc(ids_in, 16)
            sp.dma_start(rows_sb[:], rows.rearrange("(a n) -> a n", a=1).broadcast_to([P, ROWS_N])).then_inc(small_in, 16)
            sp.dma_start(bqk_sb[:], bqk).then_inc(small_in, 16)
            sp.dma_start(dl_sb[:], decay).then_inc(small_in, 16)
            sp.dma_start(wqkv_sb[:], wqkv).then_inc(small_in, 16)
            sp.dma_start(wout_sb[:], wout).then_inc(small_in, 16)
            sp.dma_start(wgate_sb[:], wgate).then_inc(small_in, 16)
            for c in range(3):
                sp.dma_start(eb3[32 * c:32 * c + 32, :], ebias).then_inc(ebias_in, 16)
            for c in range(8):
                n = E * 2 * FF // 8
                sp.dma_start(wgu_sb[:, c * n:(c + 1) * n], wgu[:, c * n:(c + 1) * n]).then_inc(experts_in, 16)
            for c in range(4):
                n = E * 2 * D // 4
                sp.dma_start(wd_sb[:, c * n:(c + 1) * n], wd[:, c * n:(c + 1) * n]).then_inc(experts_in, 16)

            for b in range(2):
                for c in range(TOP * U):
                    sp.wait_ge(rows_out[b][c], 16 * (UNITS // 2))
            sp.wait_ge(tab_ready, 2)
            sp.wait_ge(pads_out, 16 * 7)

            def load_tile(j, r, lap):
                row = sp.value_load(tab_b[0:1, bass.ds(j, 1)], min_val=0, max_val=DUMMY)
                if lap is not None:
                    sp.wait_ge(xT_made, lap)
                    sp.wait_ge(widx_ready, lap)
                sp.dma_start(xs[:, r, :], xs_dram[bass.ds(row, P), :]).then_inc(xs_in[r], 16)

            for r in range(R):
                load_tile(r, r, None)
            with sp.Fori(1, TILES // R) as t:
                for r in range(R):
                    load_tile(t * R + r, r, t * R + (r + 1 - R))

            for r in range(R):
                sp.wait_ge(y_out[r], 16 * (TILES // R))

            y_t = y_dram.rearrange("(k t p) d -> p k t d", k=TOP, p=P)

            sp.wait_ge(gu_made, TILES)
            for c in range(SEQS // CB):
                for k, (dst, arrived) in enumerate(((ya, ya_in), (yb, yb_in))):
                    sp.dma_start(dst[:, c * CB:(c + 1) * CB, :], y_t[:, k, c * CB:(c + 1) * CB, :]).then_inc(arrived[c], 16)
            sp.wait_ge(stored, 16 * (SEQS // CB))

        @block.gpsimd
        def _(pool):
            n = [0]

            def made(ins):
                n[0] += 1
                ins.then_inc(pool_const, 1)

            made(pool.memset(ident[:], 0.0))
            made(pool.memset(causal[:], 1.0))
            made(pool.memset(tri[:], 1.0))
            made(pool.memset(ones_bf[:], 1.0))
            made(pool.iota(rowno[:], [[0, 1]], base=0, channel_multiplier=1))
            made(pool.iota(padq[:], [[4, 4]], base=0, channel_multiplier=0, allow_small_or_imprecise_dtypes=True))
            made(pool.memset(pad_rows[:], 0.0))
            made(pool.memset(selp[:], 0.0))
            made(pool.iota(par_i[:], [[0, 1]], base=0, channel_multiplier=1))
            made(pool.iota(tokid[:], [[TOK, TOP], [P, SEQS]], base=0, channel_multiplier=1))
            made(pool.iota(iota_e[:], [[1, E]], base=0, channel_multiplier=0, allow_small_or_imprecise_dtypes=True))
            made(pool.iota(eoff[:], [[REG, E]], base=0, channel_multiplier=0, allow_small_or_imprecise_dtypes=True))
            made(pool.iota(tileno[:], [[0, 1]], base=0, channel_multiplier=1, allow_small_or_imprecise_dtypes=True))
            pool.wait_ge(pool_const, n[0])
            made(pool.affine_select(out=ident[:], in_=ident[:], compare_op=NOT_EQUAL, fill=1.0, base=0,
                                    pattern=[[-1, P]], channel_multiplier=1))
            made(pool.affine_select(out=causal[:], in_=causal[:], compare_op=ALU.is_ge, fill=0.0, base=0,
                                    pattern=[[1, P]], channel_multiplier=-1))
            made(pool.affine_select(out=tri[:], in_=tri[:], compare_op=ALU.is_gt, fill=0.0, base=0,
                                    pattern=[[1, P]], channel_multiplier=-1))
            made(pool.iota(pad_rows[:, :, ROW - 1].bitcast(I32), [[0, PADS]], base=SKIP, channel_multiplier=0))
            for c in range(3):
                made(pool.affine_select(out=selp[:], in_=selp[:], compare_op=NOT_EQUAL, fill=1.0, base=-32 * c,
                                        pattern=[[-1, E]], channel_multiplier=1))
                pool.wait_ge(pool_const, n[0])
            assert n[0] == CONST_POOL

            pool.wait_ge(ids_in, 16)

            pool.dma_start(xs_dram[DUMMY:DUMMY + P, :], pad_rows[:, 0, :]).then_inc(pads_out, 16)

            def gather(u, b, staged, count):
                pool.tensor_copy(ids_now[:, b, :], ids_sb[:, bass.ds(u * U, U)]).then_inc(staged, 1)
                stands_first(pool, pool_const)
                pool.wait_ge(staged, count)
                for s in range(U):
                    pool.indirect_dma_start(emb[:, b, s, :], None, wt,
                                            bass.IndirectOffsetOnAxis(ap=ids_now[:, b, s:s + 1], axis=0))\
                        .then_inc(emb_in[b][s], 16)

            def add_b(b, arrived):
                for s in range(U):
                    pool.wait_ge(emb_in[b][s], 16 * arrived)
                pool.tensor_tensor(emb[:, b, :, :], emb[:, b, :, :],
                                   rows_sb[:, None, ROW_TOKB:ROW_TOKB + D].broadcast_to([P, U, D]), ALU.add).then_inc(emb_sum, 1)

            def add_lnb(i, b):
                pool.wait_ge(h_ready, i)
                if not isinstance(i, int) or i >= 2:
                    pool.wait_ge(h2_ready, i - 1)
                pool.tensor_tensor(hlb[:], h[:, b, :, :],
                                   rows_sb[:, None, ROW_LNB:ROW_LNB + D].broadcast_to([P, U, D]), ALU.add).then_inc(hlb_ready, 1)

            def scatter(b, count):
                stands_first(pool, pool_const)
                pool.wait_ge(slot_ready[b], count)
                pool.wait_ge(w_ready[b], count)
                pool.wait_ge(rr1_ready[b], count)
                for k in range(TOP):
                    for s in range(U):
                        pool.indirect_dma_start(xs_dram, bass.IndirectOffsetOnAxis(ap=slot[:, b, k, s:s + 1], axis=0),
                                                rr[:, b, k, s, :], None).then_inc(rows_out[b][k * U + s], 16)

            def gather_static(u):
                if u <= 4:
                    gather(u, u % 2, ids_staged_first, u + 1)
                else:
                    gather(u, u % 2, ids_staged[u % 2], (u - 3) // 2)

            def step(i):
                if i + 1 < UNITS:
                    add_b((i + 1) % 2, (i + 1) // 2 + 1)
                if 1 <= i <= UNITS:
                    add_lnb(i, (i - 1) % 2)
                if i + 2 < UNITS:
                    pool.wait_ge(h_ready, i + 1)
                    gather_static(i + 2)
                if i >= 3:
                    scatter((i - 3) % 2, (i - 3) // 2 + 1)

            pool.wait_ge(small_in, 16 * 6)
            gather_static(0)
            gather_static(1)
            add_b(0, 1)
            for i in range(5):
                step(i)
            with pool.Fori(2, UNITS // 2 - 2) as t:
                for b in (1, 0):
                    i = t * 2 + (2 - b)
                    add_b(1 - b, t + 2)
                    add_lnb(i, 1 - b)
                    pool.wait_ge(h_ready, i + 1)
                    gather(i + 2, b, ids_staged[b], t)
                    scatter(1 - b, t)
            for i in range(UNITS - 3, UNITS + 3):
                step(i)

            pool.wait_ge(padidx_ready, 1)
            for k in range(4):
                pool.indirect_dma_start(xs_dram, bass.IndirectOffsetOnAxis(ap=padidx[:, k:k + 1], axis=0),
                                        pad_rows[:, 0, :], None).then_inc(pads_out, 16)
            pool.wait_ge(padidx_ready, 2)
            pool.wait_ge(pads_out, 16 * 5)
            for k in range(2):
                pool.indirect_dma_start(xs_dram.rearrange("(n a) d -> n (a d)", a=PADS),
                                        bass.IndirectOffsetOnAxis(ap=padbidx[:, k:k + 1], axis=0),
                                        pad_rows[:].rearrange("p a d -> p (a d)"), None).then_inc(pads_out, 16)

            with pool.Fori(1, TILES // R + 1) as t:
                for r in range(R):
                    stands_first(pool, pool_const)
                    pool.wait_ge(y_ready[r], t)
                    pool.indirect_dma_start(y_dram, bass.IndirectOffsetOnAxis(ap=widx[:, r, 1:2].bitcast(U32), axis=0),
                                            ysb[:, r, :], None, bounds_check=TOP * TOK - 1, oob_is_err=False)\
                        .then_inc(y_out[r], 16)

        @block.scalar
        def _(act):
            nc.scalar.preload_act_table_set("natural_log_exp_and_others")
            act.wait_ge(small_in, 16 * 6)
            nc.scalar.activation(lam[:, 0:1], dl_sb[:], ACT.Exp, scale=-1.0).then_inc(act_const, 1)
            act.wait_ge(dve_const, 1)

            def rstd(var, ln, rs, mv_ready, ln_ready, rs_ready, u):
                act.wait_ge(mv_ready, u + 1)
                nc.scalar.activation(ln[:], var[:, :, 1], ACT.Ln, bias=eps_ln[:, 0:1]).then_inc(ln_ready, 1)
                act.wait_ge(ln_ready, u + 1)
                nc.scalar.activation(rs[:], ln[:], ACT.Exp, scale=-0.5).then_inc(rs_ready, 1)

            def make_h(u, b):
                act.wait_ge(emb_sum, u + 1)
                if later(u, 2):
                    act.wait_ge(hlb_ready, u - 1)
                nc.scalar.activation(h[:, b, :, :], emb[:, b, :, :], ACT.Copy, scale=EMB_SCALE).then_inc(h_ready, 1)

            def later(i, k):
                return not isinstance(i, int) or i >= k

            def step(i, b, norm, first, second, third):
                c = 1 - b
                if third:
                    rstd(mv3, ln3, rs3, mv3_ready, ln3_ready, rs3_ready, i - 2)
                if norm:
                    make_h(i + 1, c)
                if third:
                    act.wait_ge(nm3_ready, i - 1)
                    if later(i, 4):
                        for q in range(TOP * U):
                            if b == 0:
                                act.wait_ge(rows_out[b][q], 8 * i - 16)
                            else:
                                act.wait_ge(rows_out[b][q], 8 * i - 24)
                    for s in range(U):
                        ins = nc.scalar.activation(rr[:, b, 0, s, 0:D],
                                                   h2[:, bass.ds(i * U + (s - 2 * U), 1), :].rearrange("p a d -> p (a d)"),
                                                   ACT.Identity, bias=nm3[:, s:s + 1], scale=rs3[:, s:s + 1])
                    ins.then_inc(rr0_ready, 1)
                    act.wait_ge(x2T_made, i - 1)
                    nc.scalar.activation(x2T[:], x2T_ps, ACT.Copy).then_inc(x2T_ready, 1)
                if norm:
                    rstd(mv1, ln1, rs1, mv1_ready, ln1_ready, rs1_ready, i + 1)
                    act.wait_ge(nm1_ready, i + 2)
                    if later(i, 0):
                        act.wait_ge(xnT_made, i + 1)
                    for s in range(U):
                        ins = nc.scalar.activation(xn[:, s, :], h[:, c, s, :], ACT.Identity, bias=nm1[:, s:s + 1],
                                                   scale=rs1[:, s:s + 1])
                    ins.then_inc(xn_ready, 1)
                if first:
                    act.wait_ge(qk_made, i + 1)
                    if later(i, 1):
                        act.wait_ge(qk_ready, i)
                    for q in range(2):
                        nc.scalar.activation(relu_qk[:, q, :], qk_ps[:, q * W:(q + 1) * W], ACT.Relu,
                                             bias=bqk_sb[:, q:q + 1]).then_inc(act_qk, 1)
                        nc.scalar.activation(exp_qk[:, q, :], qk_ps[:, q * W:(q + 1) * W], ACT.Exp,
                                             bias=bqk_sb[:, q:q + 1]).then_inc(act_qk, 1)
                    act.wait_ge(v_made, i + 1)
                    if later(i, 2):
                        act.wait_ge(nd_made, i - 1)
                    for s in range(U):
                        ins = nc.scalar.activation(vx[:, b, s, :, 0:HD],
                                                   v_ps[:, s * D:(s + 1) * D].rearrange("p (a f) -> p a f", f=HD), ACT.Copy)
                    ins.then_inc(v_ready, 1)
                if third:
                    act.wait_ge(ls_ready, 2 * i - 2)
                    nc.scalar.activation(es[:], ls[:], ACT.Exp).then_inc(es_ready, 1)
                    act.wait_ge(rr0_ready, i - 1)
                    nc.scalar.activation(rr[:, b, 1, :, 0:D], rr[:, b, 0, :, 0:D], ACT.Copy).then_inc(rr1_ready[b], 1)
                if norm:
                    act.wait_ge(xnT_made, i + 2)
                    nc.scalar.activation(xnT[:], xnT_ps, ACT.Copy).then_inc(xnT_ready, 1)
                if second:
                    act.wait_ge(oT_made, i)
                    nc.scalar.activation(oT[:], oT_ps, ACT.Copy).then_inc(oT_ready, 1)
                if first:
                    act.wait_ge(qd_ready, i + 1)
                    if later(i, 1):
                        act.wait_ge(sc_made, 4 * i)
                    for g in range(2, 4):
                        rows_g = slice(32 * g, 32 * g + 32)
                        for q in range(2):
                            ins = nc.scalar.activation(qz[rows_g, :, g, q, :], qd[rows_g, :].rearrange("p (s l) -> p s l", l=P),
                                                       ACT.Copy, scale=par[rows_g, q:q + 1])
                    ins.then_inc(qeo_ready, 1)
                if second:
                    rstd(mv2, ln2, rs2, mv2_ready, ln2_ready, rs2_ready, i - 1)
                    act.wait_ge(nm2_ready, i)
                    if later(i, 2):
                        act.wait_ge(aog_ready, i - 1)
                    for s in range(U):
                        ins = nc.scalar.activation(aon[:, s, :], ao_ps[:, s * D:(s + 1) * D], ACT.Identity,
                                                   bias=nm2[:, s:s + 1], scale=rs2[:, s:s + 1])
                    ins.then_inc(aon_ready, 1)

            skewed(act, step)

            nc.scalar.preload_act_table(ACT.Silu)

            def evac_xT(j, r):
                act.wait_ge(xT_made, j + 1)
                if not isinstance(j, int) or j >= R:
                    act.wait_ge(gu_made, j - (R - 1))
                nc.scalar.activation(xT[:, r % R, :], xT_ps[r % 2], ACT.Copy).then_inc(xT_ready, 1)

            def silu(j, r):
                act.wait_ge(gu_made, j + 1)
                if not isinstance(j, int) or j >= 2:
                    act.wait_ge(hh_ready, j - 1)
                nc.scalar.activation(sg[:, r % 2, :], gu_ps[r % 2][:, 0:FF], ACT.Silu).then_inc(sg_ready, 1)

            evac_xT(0, 0)
            with act.Fori(0, TILES // R - 1) as t:
                for r in range(R):
                    evac_xT_j = t * R + (r + 1)
                    act.wait_ge(xT_made, evac_xT_j + 1)
                    nc.scalar.activation(xT[:, (r + 1) % R, :], xT_ps[(r + 1) % 2], ACT.Copy).then_inc(xT_ready, 1)
                    act.wait_ge(gu_made, t * R + (r + 1))
                    nc.scalar.activation(sg[:, r % 2, :], gu_ps[r % 2][:, 0:FF], ACT.Silu).then_inc(sg_ready, 1)
            for j in range(TILES - R, TILES):
                if j + 1 < TILES:
                    evac_xT(j + 1, j + 1)
                silu(j, j)

            out_t = out.rearrange("(t p) d -> p t d", p=P)
            for c in range(SEQS // CB):
                act.wait_ge(sum_ready, c + 1)
                act.dma_start(out_t[:, c * CB:(c + 1) * CB, :], yb[:, c * CB:(c + 1) * CB, :]).then_inc(stored, 16)

        @block.vector
        def _(dve):
            V = nc.vector
            n = [0]

            def link(ins):
                n[0] += 1
                ins.then_inc(dve_const, 1)
                dve.wait_ge(dve_const, n[0])

            V.memset(eps_ln[:], LN_EPS)
            V.memset(vx[:], 1.0)
            V.memset(qz[:], 0.0)
            V.memset(cum[:, 1, :], 0.0)
            V.memset(onesf[:], 1.0)
            V.memset(decq[:, 0:1], 1.0)
            link(V.memset(bias_bf[:], 0.0))
            dve.wait_ge(act_const, 1)
            link(V.tensor_scalar_add(lam[:, 0:1], lam[:, 0:1], 1.0))
            link(V.reciprocal(lam[:, 1:2], lam[:, 0:1]))
            link(V.tensor_scalar(lam[:, 0:1], lam[:, 1:2], 0.01, 0.99, ALU.mult, ALU.add))
            for c in range(7):
                m = 1 << c
                link(V.tensor_scalar(decq[:, m:2 * m], decq[:, 0:m], lam[:, c % 2:c % 2 + 1], None, ALU.mult))
                link(V.tensor_tensor(lam[:, (c + 1) % 2:(c + 1) % 2 + 1], lam[:, c % 2:c % 2 + 1],
                                     lam[:, c % 2:c % 2 + 1], ALU.mult))
            link(V.reciprocal(deck[:], decq[:]))
            dve.wait_ge(pool_const, CONST_POOL)
            link(V.tensor_scalar(par_i[:], par_i[:], 4, 1, ALU.logical_shift_right, ALU.bitwise_and))
            link(V.tensor_copy(par[:, 1:2], par_i[:]))
            link(V.tensor_scalar(par[:, 0:1], par[:, 1:2], -1.0, 1.0, ALU.mult, ALU.add))
            link(V.tensor_scalar_mul(decq[:], decq[:], 1.0 / float(HD) ** 0.5))
            for q in range(2):
                link(V.tensor_scalar(decqm[:, q, :], decq[:], par[:, q:q + 1], None, ALU.mult))

            dve.wait_ge(ebias_in, 48)
            q = slice(0, 96)
            link(V.tensor_copy(ebm[q, :], eb3[q, :]))
            V.tensor_copy(bias_bf[0:32, :], ebm[0:32, :])
            link(V.tensor_tensor(eb3[q, :], eb3[q, :], ebm[q, :], ALU.subtract))
            link(V.tensor_copy(ebm[q, :], eb3[q, :]))
            V.tensor_copy(bias_bf[32:64, :], ebm[32:64, :])
            link(V.tensor_tensor(eb3[q, :], eb3[q, :], ebm[q, :], ALU.subtract))
            link(V.tensor_copy(bias_bf[64:96, :], eb3[64:96, :]))
            V.tensor_copy(sel[:], selp[:, :, None].broadcast_to([P, E, P])).then_inc(bias_ready, 1)

            link(V.tensor_scalar(pad_i[:, 0:1], rowno[:], 2, None, ALU.logical_shift_right))
            link(V.tensor_scalar(pad_i[:, 1:2], rowno[:], 3, None, ALU.bitwise_and))
            link(V.tensor_copy(pad_e[:], pad_i[:, 0:1]))
            link(V.tensor_copy(pad_q[:], pad_i[:, 1:2]))
            link(V.tensor_scalar(padsel[:], iota_e[:], pad_e[:, 0:1], None, ALU.is_equal))
            link(V.tensor_scalar(padq[:], padq[:], pad_q[:, 0:1], None, ALU.add))

            lng = rows_sb[:, None, ROW_LNG:ROW_LNG + D].broadcast_to([P, U, D])
            bgate = rows_sb[:, None, ROW_BGATE:ROW_BGATE + E].broadcast_to([P, U, E])

            def stats(src, st, mv, st_ready, mv_ready, u):
                for s in range(U):
                    ins = V.bn_stats(st[:, s, :], src(s))
                ins.then_inc(st_ready, 1)
                stands_first(dve, bias_ready)
                dve.wait_ge(st_ready, u)
                for s in range(U):
                    ins = V.bn_aggr(mv[:, s, :], st[:, s, :])
                ins.then_inc(mv_ready, 1)

            def later(i, k):
                return not isinstance(i, int) or i >= k

            def negmean(nm, mv, rs, rs_ready, nm_ready, u):
                dve.wait_ge(rs_ready, u)
                V.scalar_tensor_tensor(out=nm[:], in0=mv[:, :, 0], scalar=-1.0, in1=rs[:], op0=ALU.mult,
                                       op1=ALU.mult).then_inc(nm_ready, 1)

            def step(i, b, norm, first, second, third):
                c = 1 - b
                if third:
                    dve.wait_ge(h2_ready, i - 1)
                    stats(lambda s: h2[:, bass.ds(i * U + (s - 2 * U), 1), :].rearrange("p a d -> p (a d)"),
                          st3, mv3, st3_ready, mv3_ready, i - 1)
                if second:
                    mask(0, i - 1)
                if third:
                    negmean(nm3, mv3, rs3, rs3_ready, nm3_ready, i - 1)
                if second:
                    mask(1, i - 1)
                if norm:
                    dve.wait_ge(h_ready, i + 2)
                    stats(lambda s: h[:, c, s, :], st1, mv1, st1_ready, mv1_ready, i + 2)
                if second:
                    mask(2, i - 1)
                if norm:
                    negmean(nm1, mv1, rs1, rs1_ready, nm1_ready, i + 2)
                if second:
                    mask(3, i - 1)
                if third:
                    dve.wait_ge(lg_made, i - 1)
                    V.tensor_tensor(lg[:], lg_ps.rearrange("p (s e) -> p s e", e=E), bgate, ALU.add).then_inc(lg_ready, 1)
                    stands_first(dve, bias_ready)
                    dve.wait_ge(lg_ready, i - 1)
                    for s in range(U):
                        V.max(mx[:, s, :], lg[:, s, :]).then_inc(mx_ready, 1)
                    dve.wait_ge(mx_ready, 2 * i - 2)
                    m1 = mx[:, :, 0:1]
                    V.tensor_tensor(ls[:, :, 0:E], lg[:], m1.broadcast_to([P, U, E]), ALU.subtract).then_inc(ls_ready, 1)
                    V.tensor_tensor(ls[:, :, E:E + TOP], mx[:, :, 0:TOP], m1.broadcast_to([P, U, TOP]),
                                    ALU.subtract).then_inc(ls_ready, 1)
                    for s in range(U):
                        V.max_index(mi[:, s, :], mx[:, s, :], lg[:, s, :]).then_inc(mi_ready, 1)
                if first:
                    dve.wait_ge(act_qk, 4 * i + 4)
                    V.scalar_tensor_tensor(out=qk[:], in0=exp_qk[:], scalar=1.0, in1=relu_qk[:],
                                           op0=ALU.min, op1=ALU.add).then_inc(qk_ready, 1)
                if third:
                    dve.wait_ge(mi_ready, 2 * i - 2)
                    V.tensor_copy(mif[:], mi[:, :, 0:TOP]).then_inc(mif_ready, 1)
                if first:
                    dve.wait_ge(qk_ready, i + 1)
                    if later(i, 1):
                        dve.wait_ge(qeo_ready, i)
                    hi = slice(P // 2, P)
                    V.tensor_tensor(qd[hi, :].rearrange("p (s l) -> p s l", l=P),
                                    qk[hi, 0, :].rearrange("p (s l) -> p s l", l=P),
                                    decq[hi, None, :].broadcast_to([P // 2, U, P]), ALU.mult).then_inc(qd_ready, 1)
                    if later(i, 1):
                        dve.wait_ge(sc_made, 4 * i)
                    for g in range(2):
                        rows_g = slice(32 * g, 32 * g + 32)
                        ins = V.tensor_tensor(qz[rows_g, :, g, :, :],
                                              qk[rows_g, 0, :].rearrange("p (s q l) -> p s q l", q=1, l=P).broadcast_to([32, U, 2, P]),
                                              decqm[rows_g, None, :, :].broadcast_to([32, U, 2, P]), ALU.mult)
                    ins.then_inc(qz_ready, 1)
                    V.tensor_tensor(kd[:, b, :].rearrange("p (s l) -> p s l", l=P),
                                    qk[:, 1, :].rearrange("p (s l) -> p s l", l=P),
                                    deck[:, None, :].broadcast_to([P, U, P]), ALU.mult).then_inc(kd_ready, 1)
                if third:
                    dve.wait_ge(mif_ready, i - 1)
                    for k in range(TOP):
                        V.tensor_tensor(mk[:, k, :, :], iota_e[:, None, :].broadcast_to([P, U, E]),
                                        mif[:, :, k:k + 1].broadcast_to([P, U, E]), ALU.is_equal).then_inc(mk_ready, 1)
                    dve.wait_ge(mk_ready, 2 * i - 2)
                    V.tensor_tensor(msum[:], mk[:, 0, :, :], mk[:, 1, :, :], ALU.add).then_inc(msum_ready, 1)
                if second:
                    dve.wait_ge(nd_made, i)
                    V.tensor_scalar_add(den[:], nd_ps[:, :, HD], DEN_EPS).then_inc(den_ready, 1)
                    dve.wait_ge(den_ready, i)
                    V.reciprocal(rec[:], den[:]).then_inc(rec_ready, 1)
                    dve.wait_ge(rec_ready, i)
                    V.tensor_tensor(o[:].rearrange("p s (a f) -> p (s a) f", f=HD), nd_ps[:, :, 0:HD],
                                    rec[:, :, None].broadcast_to([P, U * HEADS, HD]), ALU.mult).then_inc(o_ready, 1)
                if third:
                    dve.wait_ge(es_ready, i - 1)
                    V.tensor_reduce(ssum[:], es[:, :, 0:E], AXX, ALU.add).then_inc(ssum_ready, 1)
                    dve.wait_ge(rr0_ready, i - 1)
                    V.tensor_copy(rr[:, b, :, :, D + 1].bitcast(I32), tokid[:, :, bass.ds(i * U - 2 * U, U)])
                    dve.wait_ge(ssum_ready, i - 1)
                    V.reciprocal(rsum[:], ssum[:]).then_inc(rsum_ready, 1)
                    dve.wait_ge(rk_made, i - 1)
                    V.tensor_tensor(rank[:], rk_ps.rearrange("p (s e) -> p s e", e=E),
                                    eoff[:, None, :].broadcast_to([P, U, E]), ALU.add).then_inc(rank_ready, 1)
                    dve.wait_ge(rsum_ready, i - 1)
                    V.tensor_tensor(rr[:, b, :, :, D].rearrange("p k s -> p s k"), es[:, :, E:E + TOP],
                                    rsum[:, :, None].broadcast_to([P, U, TOP]), ALU.mult).then_inc(w_ready[b], 1)
                    V.tensor_tensor(mpair[:], msum[:, 0, :], msum[:, 1, :], ALU.add).then_inc(mpair_ready, 1)
                    dve.wait_ge(rank_ready, i - 1)
                    for k in range(TOP):
                        V.tensor_tensor(slotp[:, k, :, :], rank[:], mk[:, k, :, :], ALU.mult).then_inc(slotp_ready, 1)
                    dve.wait_ge(mpair_ready, i - 1)
                    V.tensor_tensor(cum[:, b, :], cum[:, c, :], mpair[:], ALU.add).then_inc(cum_ready, 1)
                if second:
                    dve.wait_ge(ao_made, i)
                    stats(lambda s: ao_ps[:, s * D:(s + 1) * D], st2, mv2, st2_ready, mv2_ready, i)
                if third:
                    dve.wait_ge(slotp_ready, 2 * i - 2)
                    V.tensor_reduce(slotf[:], slotp[:], AXX, ALU.add).then_inc(slotf_ready, 1)
                if second:
                    negmean(nm2, mv2, rs2, rs2_ready, nm2_ready, i)
                if second:
                    dve.wait_ge(aon_ready, i)
                    V.tensor_tensor(aog[:], aon[:], lng, ALU.mult).then_inc(aog_ready, 1)
                if third:
                    dve.wait_ge(slotf_ready, i - 1)
                    V.tensor_copy(slot[:, b, :, :], slotf[:]).then_inc(slot_ready[b], 1)
                if second:
                    dve.wait_ge(aog_ready, i)
                    dve.wait_ge(hlb_ready, i)
                    V.tensor_tensor(h2[:, bass.ds(i * U - U, U), :], aog[:], hlb[:], ALU.add).then_inc(h2_ready, 1)

            def mask(g, u):
                dve.wait_ge(sc_made, u * 4 + (g + 1))
                if later(u, 1):
                    dve.wait_ge(nd_made, u)
                V.tensor_tensor(sm[:, g, :, :], sc_ps[g][:].rearrange("p (a l) -> p a l", l=P),
                                causal[:, None, :].broadcast_to([P, 2 * U, P]), ALU.mult).then_inc(sm_ready, 1)

            skewed(dve, step)

            k = [0]

            def tstep(ins):
                k[0] += 1
                ins.then_inc(tab_step, 1)
                dve.wait_ge(tab_step, k[0])

            dve.wait_ge(cnt_made, 1)
            tstep(V.tensor_copy(cnt[:], cnt_ps))
            tstep(V.tensor_tensor(padrow_f[:], cnt[:], eoff[:], ALU.add))
            tstep(V.tensor_tensor(padrow_f[:], padrow_f[:], padsel[:], ALU.mult))
            tstep(V.tensor_reduce(padbase[:], padrow_f[:], AXX, ALU.add))
            V.tensor_scalar(padidx[:], padq[:], padbase[:, 0:1], None, ALU.add).then_inc(padidx_ready, 1)
            tstep(V.tensor_scalar_add(padblk[:], padbase[:], float(PADS - 1)))
            tstep(V.tensor_copy(padblk_i[:], padblk[:]))
            tstep(V.tensor_scalar(padblk_i[:], padblk_i[:], 4, None, ALU.logical_shift_right))
            tstep(V.tensor_copy(padblk[:], padblk_i[:]))
            V.tensor_scalar(padbidx[:], padq[:, 0:2], padblk[:, 0:1], None, ALU.add).then_inc(padidx_ready, 1)
            tstep(V.tensor_scalar_add(cnt[:], cnt[:], float(P - 1)))
            tstep(V.tensor_copy(cnt_i[:], cnt[:]))
            tstep(V.tensor_scalar(nt_i[:], cnt_i[:], 7, None, ALU.logical_shift_right))
            tstep(V.tensor_copy(ntf[:], nt_i[:]))
            tstep(V.tensor_tensor_scan(endt[:], onesf[:], ntf[:], 0.0, ALU.mult, ALU.add))
            tstep(V.tensor_scalar(passed[:], endt[:], tileno[:, 0:1], None, ALU.is_le))
            tstep(V.tensor_tensor(passn[:], passed[:], ntf[:], ALU.mult))
            tstep(V.tensor_reduce(tab[:, 0:1], passed[:], AXX, ALU.add))
            tstep(V.tensor_reduce(tab[:, 1:2], passn[:], AXX, ALU.add))
            tstep(V.tensor_tensor(tab[:, 1:2], tileno[:], tab[:, 1:2], ALU.subtract))
            tstep(V.tensor_scalar_mul(tab[:, 2:3], tab[:, 0:1], float(REG)))
            tstep(V.tensor_scalar_mul(tab[:, 1:2], tab[:, 1:2], float(P)))
            tstep(V.tensor_tensor(tab[:, 1:2], tab[:, 1:2], tab[:, 2:3], ALU.add))
            tstep(V.tensor_scalar_min(tab[:, 1:2], tab[:, 1:2], float(DUMMY)))
            tstep(V.tensor_scalar_min(tab[:, 0:1], tab[:, 0:1], float(E - 1)))
            assert k[0] == TAB_STEPS
            dve.wait_ge(tab_made, 1)
            V.tensor_copy(tab_e[:], tab_ps[0:1, 0:TILES]).then_inc(tab_ready, 1)
            V.tensor_copy(tab_b[:], tab_ps[0:1, P:P + TILES]).then_inc(tab_ready, 1)

            def copy_widx(t, r):
                j = t * R + r
                dve.wait_ge(xs_in[r % R], lap(t, r) * 16)
                if later(j, R):
                    dve.wait_ge(y_out[r % R], lap(t, r) * 16 - 16)
                V.tensor_copy(widx[:, r % R, :], xs[:, r % R, D:D + 2]).then_inc(widx_ready, 1)

            def gate(t, r):
                j = t * R + r
                dve.wait_ge(sg_ready, j + 1)
                if later(j, 2):
                    dve.wait_ge(hT_made, j - 1)
                V.tensor_tensor(hh[:, r % 2, :], gu_ps[r % 2][:, FF:2 * FF], sg[:, r % 2, :], ALU.mult).then_inc(hh_ready, 1)

            def evac_hT(t, r):
                j = t * R + r
                dve.wait_ge(hT_made, j + 1)
                if later(j, 2):
                    dve.wait_ge(y_made, j - 1)
                V.tensor_copy(hT[:, r % 2, :], hT_ps[r % 2]).then_inc(hT_ready, 1)

            def evac_y(t, r):
                j = t * R + r
                dve.wait_ge(y_made, j + 1)
                V.tensor_scalar(ysb[:, r % R, :], y_ps[r % 2], widx[:, r % R, 0:1], None, ALU.mult).then_inc(y_ready[r % R], 1)

            def estep(t, r, full):
                if full or r + 1 < TILES:
                    copy_widx(t, r + 1)
                if full or r < TILES:
                    gate(t, r)
                if full or 0 <= r - 1 < TILES:
                    evac_hT(t, r - 1)
                if full or 0 <= r - 2 < TILES:
                    evac_y(t, r - 2)

            copy_widx(0, 0)
            for j in range(R):
                estep(0, j, False)
            with dve.Fori(1, TILES // R - 1) as t:
                for r in range(R):
                    estep(t, r, True)
            for j in range(TILES - R, TILES + 2):
                estep(0, j, False)

            for c in range(SEQS // CB):
                q = slice(c * CB, (c + 1) * CB)
                dve.wait_ge(ya_in[c], 16)
                dve.wait_ge(yb_in[c], 16)
                V.tensor_tensor(ya[:, q, :], ya[:, q, :], h2[:, q, :], ALU.add).then_inc(sum1_ready, 1)
                dve.wait_ge(sum1_ready, c + 1)
                V.tensor_tensor(yb[:, q, :], ya[:, q, :], yb[:, q, :], ALU.add).then_inc(sum_ready, 1)

        @block.tensor
        def _(pe):
            M = nc.tensor.matmul

            def later(i, k):
                return not isinstance(i, int) or i >= k

            pe.wait_ge(small_in, 16 * 6)
            pe.wait_ge(pool_const, CONST_POOL)
            pe.wait_ge(bias_ready, 1)

            def step(i, b, norm, first, second, third):
                c = 1 - b
                if second:
                    pe.wait_ge(kd_ready, i)
                    pe.wait_ge(qz_ready, i)
                    pe.wait_ge(qeo_ready, i)
                    if later(i, 2):
                        pe.wait_ge(sm_ready, 4 * i - 4)
                    for g in range(4):
                        for s in range(U):
                            ins = M(sc_ps[g][:, s * 2 * P:(s + 1) * 2 * P], kd[:, c, s * P:(s + 1) * P],
                                    qz[:, s, g, :, :].rearrange("p q l -> p (q l)"), start=True, stop=True)
                        ins.then_inc(sc_made, 1)
                if third:
                    pe.wait_ge(rr0_ready, i - 1)
                    if later(i, 3):
                        pe.wait_ge(rank_ready, i - 2)
                    for s in range(U):
                        ins = nc.tensor.transpose(x2T_ps[:, s * P:(s + 1) * P], rr[:, b, 0, s, 0:D], ident[:])
                    ins.then_inc(x2T_made, 1)
                if first:
                    pe.wait_ge(xnT_ready, i + 1)
                    if later(i, 1):
                        pe.wait_ge(act_qk, 4 * i)
                    M(qk_ps[:, 0:W], wqkv_sb[:, 0:D], xnT[:], start=True, stop=True)
                    M(qk_ps[:, W:2 * W], wqkv_sb[:, D:2 * D], xnT[:], start=True, stop=True).then_inc(qk_made, 1)
                    for s in range(U):
                        M(v_ps[:, s * D:(s + 1) * D], xnT[:, s * P:(s + 1) * P], wqkv_sb[:, 2 * D:3 * D],
                          start=True, stop=False)
                        ins = M(v_ps[:, s * D:(s + 1) * D], ones_bf[0:96, :], bias_bf[0:96, BIAS_N:BIAS_N + D],
                                start=False, stop=True)
                    ins.then_inc(v_made, 1)
                if third:
                    pe.wait_ge(x2T_ready, i - 1)
                    for s in range(U):
                        ins = M(lg_ps[:, s * E:(s + 1) * E], x2T[:, s * P:(s + 1) * P], wgate_sb[:], start=True, stop=True)
                    ins.then_inc(lg_made, 1)
                if second:
                    pe.wait_ge(v_ready, i)
                    if later(i, 2):
                        pe.wait_ge(aon_ready, i - 1)
                    for g in range(4):
                        pe.wait_ge(sm_ready, 4 * i + (g - 3))
                        for s in range(U):
                            for q in range(2):
                                ins = M(nd_ps[:, s * HEADS + 2 * g + q, :], sm[:, g, 2 * s + q, :],
                                        vx[:, c, s, 2 * g + q, :], start=True, stop=True)
                    ins.then_inc(nd_made, 1)
                if norm:
                    pe.wait_ge(xn_ready, i + 2)
                    if later(i, 0):
                        pe.wait_ge(v_ready, i + 1)
                    for s in range(U):
                        ins = nc.tensor.transpose(xnT_ps[:, s * P:(s + 1) * P], xn[:, s, :], ident[:])
                    ins.then_inc(xnT_made, 1)
                if third:
                    pe.wait_ge(msum_ready, i - 1)
                    pe.wait_ge(lg_ready, i - 1)
                    if later(i, 3):
                        pe.wait_ge(cum_ready, i - 2)
                    M(rk_ps, tri[:], msum[:].rearrange("p s e -> p (s e)"), start=True, stop=False)
                    M(rk_ps.rearrange("p (s e) -> p s e", e=E), ones_bf[:], cum[:, c:c + 1, :].broadcast_to([P, U, E]), start=False, stop=False)
                    M(rk_ps[:, E:2 * E], ones_bf[:], msum[:, 0, :], start=False, stop=True).then_inc(rk_made, 1)
                if second:
                    pe.wait_ge(o_ready, i)
                    for s in range(U):
                        ins = nc.tensor.transpose(oT_ps[:, s * P:(s + 1) * P], o[:, s, :], ident[:])
                    ins.then_inc(oT_made, 1)
                if second:
                    pe.wait_ge(oT_ready, i)
                    for s in range(U):
                        M(ao_ps[:, s * D:(s + 1) * D], oT[:, s * P:(s + 1) * P], wout_sb[:], start=True, stop=False)
                        ins = M(ao_ps[:, s * D:(s + 1) * D], ones_bf[0:96, :], bias_bf[0:96, BIAS_N + D:BIAS_N + 2 * D],
                                start=False, stop=True)
                    ins.then_inc(ao_made, 1)

            skewed(pe, step)

            pe.wait_ge(cum_ready, UNITS)
            pe.wait_ge(rank_ready, UNITS)
            M(cnt_ps, ones_bf[:], cum[:, (UNITS + 1) % 2, :], start=True, stop=True).then_inc(cnt_made, 1)
            pe.wait_ge(tab_step, TAB_STEPS)
            for q in range(2):
                ins = M(tab_ps[0:1, q * P:(q + 1) * P], tab[:, q:q + 1], ident[:], start=True, stop=True)
            ins.then_inc(tab_made, 1)
            pe.wait_ge(tab_ready, 2)
            pe.wait_ge(experts_in, 16 * 12)

            def trans_x(t, r):
                j = t * R + r
                pe.wait_ge(xs_in[r % R], lap(t, r) * 16)
                if later(j, 2):
                    pe.wait_ge(xT_ready, j - 1)
                nc.tensor.transpose(xT_ps[r % 2], xs[:, r % R, 0:D], ident[:]).then_inc(xT_made, 1)

            def expert(t, r):
                return pe.value_load(tab_e[0:1, bass.ds(t * R + r, 1)], min_val=0, max_val=E - 1)

            def gate_up(t, r, e):
                j = t * R + r
                pe.wait_ge(xT_ready, j + 1)
                if later(j, 2):
                    pe.wait_ge(hh_ready, j - 1)
                M(gu_ps[r % 2][:], xT[:, r % R, :], wgu_sb[:, bass.ds(e * (2 * FF), 2 * FF)], start=True, stop=False)
                M(gu_ps[r % 2][:], sel[:, bass.ds(e, 1), :].rearrange("p a t -> p (a t)"), bias_bf[:, 0:2 * FF],
                  start=False, stop=True).then_inc(gu_made, 1)

            def trans_h(t, r):
                j = t * R + r
                pe.wait_ge(hh_ready, j + 1)
                if later(j, 2):
                    pe.wait_ge(hT_ready, j - 1)
                for q in range(2):
                    ins = nc.tensor.transpose(hT_ps[r % 2][:, q * P:(q + 1) * P], hh[:, r % 2, q * P:(q + 1) * P], ident[:])
                ins.then_inc(hT_made, 1)

            def down(t, r, e):
                j = t * R + r
                pe.wait_ge(hT_ready, j + 1)
                if later(j, 2):
                    pe.wait_ge(y_ready[(r - 2) % R], lap(t, r - 2))
                for q in range(2):
                    M(y_ps[r % 2], hT[:, r % 2, q * P:(q + 1) * P], wd_sb[:, bass.ds(e * (2 * D) + q * D, D)],
                      start=(q == 0), stop=False)
                M(y_ps[r % 2], sel[:, bass.ds(e, 1), :].rearrange("p a t -> p (a t)"), bias_bf[:, 2 * FF:BIAS_N],
                  start=False, stop=True).then_inc(y_made, 1)

            def estep(t, r, full, e, first, last):
                if full or r + 1 < TILES:
                    trans_x(t, r + 1)
                if full or r < TILES:
                    gate_up(t, r, e[r])
                if full or 0 <= r - 1 < TILES:
                    trans_h(t, r - 1)
                if r + 1 < last:
                    e[r + 1] = expert(t, r + 1)
                if full or 0 <= r - 2 < TILES:
                    if r - 2 < first:
                        e[r - 2] = expert(t, r - 2)
                    down(t, r - 2, e[r - 2])

            trans_x(0, 0)
            e = {0: expert(0, 0)}
            for j in range(R):
                estep(0, j, False, e, 0, R)
            with pe.Fori(1, TILES // R - 1) as t:
                e = {0: expert(t, 0)}
                for r in range(R):
                    estep(t, r, True, e, 0, R)
            e = {TILES - R: expert(0, TILES - R)}
            for j in range(TILES - R, TILES + 2):
                estep(0, j, False, e, TILES - R, TILES)


def kernel(**inputs):
    import numpy as np
    import concourse.bacc as bacc
    from concourse.bass_utils import run_bass_kernel_spmd

    a = {k: np.ascontiguousarray(v) for k, v in inputs.items()}
    b_qkv = a["L0_attn_b_qkv"]
    attn_bias = np.zeros((E, 2 * D), np.float32)
    attn_bias[0, :D] = b_qkv[2 * D:]
    attn_bias[0, D:] = a["L0_attn_b_out"]
    arrays = {
        "ids": np.ascontiguousarray(a["x"].T).view(np.uint32),
        "wt": np.ascontiguousarray(a["L0_tok_W"].T),
        "rows": np.concatenate([a["L0_tok_b"], b_qkv[2 * D:], a["L0_attn_b_out"], a["L0_attn_ln_g"],
                                a["L0_attn_ln_b"], a["L0_ffn_bgate"]]),
        "bqk": np.ascontiguousarray(b_qkv[:2 * D].reshape(2, D).T),
        "decay": np.ascontiguousarray(np.broadcast_to(a["L0_attn_decay_logits"][:, None], (HEADS, HD)).reshape(D, 1)),
        "wqkv": a["L0_attn_W_qkv"],
        "wout": a["L0_attn_W_out"],
        "wgate": a["L0_ffn_Wgate"],
        "wgu": np.ascontiguousarray(np.concatenate([a["L0_ffn_Wg"], a["L0_ffn_Wu"]], axis=2).transpose(1, 0, 2)
                                    .reshape(P, E * 2 * FF)),
        "wd": np.ascontiguousarray(a["L0_ffn_Wd"].reshape(E, 2, P, D).transpose(2, 0, 1, 3).reshape(P, E * 2 * D)),
        "ebias": np.concatenate([a["L0_ffn_bg"], a["L0_ffn_bu"], a["L0_ffn_bd"], attn_bias], axis=1),
    }
    nc = bacc.Bacc("TRN2", target_bir_lowering=False, num_devices=1)
    args = [nc.dram_tensor(k, v.shape, mybir.dt.from_np(v.dtype), kind="ExternalInput").ap() for k, v in arrays.items()]
    args.append(nc.dram_tensor("out", (TOK, D), F32, kind="ExternalOutput").ap())
    build(nc, *args)
    r = run_bass_kernel_spmd(nc, [arrays], core_ids=[0])
    return r.results[0]["out"].reshape(SEQS, P, D)
```

```python
from contextlib import ExitStack

import concourse.bass as bass
from concourse import mybir

F32 = mybir.dt.float32
BF16 = mybir.dt.bfloat16
I32 = mybir.dt.int32
U32 = mybir.dt.uint32
ALU = mybir.AluOpType
ACT = mybir.ActivationFunctionType
AXX = mybir.AxisListType.X
NOT_EQUAL = ALU.not_equal

P = 128
SEQS = 32
D = 128
HEADS = 8
HD = D // HEADS
E = 32
FF = 256
TOP = 2
TOK = SEQS * P
U = 2
UNITS = SEQS // U
W = U * P
REG = TOK + P
TILES = TOP * TOK // P + E
ROW = D + 2
DUMMY = E * REG
SKIP = 1 << 20
LN_EPS = 1e-5
DEN_EPS = 1e-6
EMB_SCALE = float(D) ** 0.5
ROW_TOKB, ROW_BV, ROW_BOUT, ROW_LNG, ROW_LNB, ROW_BGATE = (D * i for i in range(6))
ROWS_N = 5 * D + E
PAD_LANES = P // E
PADS = P // PAD_LANES
PIECES = ROW // 2
VC = 32
BIAS_N = 2 * FF + D


def build(nc, ids, wt, rows, bqk, decay, wqkv, wout, wgate, wgu, wd, ebias, out):
    ctx = ExitStack()
    with ctx:
        def sb(name, shape, dt=F32):
            return ctx.enter_context(nc.sbuf_tensor(name, shape, dt))

        def ps(name, shape, dt=F32):
            return ctx.enter_context(nc.psum_tensor(name, shape, dt))

        def sem(name):
            return ctx.enter_context(nc.semaphore(name))

        xs_dram = nc.dram_tensor("dispatched_rows", [E * REG + P, ROW], F32, kind="Internal").ap()
        y_dram = nc.dram_tensor("expert_rows", [TOP * TOK, D], F32, kind="Internal").ap()

        wgu_sb = sb("wgu_sb", [P, E * 2 * FF])
        wd_sb = sb("wd_sb", [P, E * 2 * D])
        wqkv_sb = sb("wqkv_sb", [P, 3 * D])
        wout_sb = sb("wout_sb", [P, D])
        wgate_sb = sb("wgate_sb", [P, E])
        rows_sb = sb("rows_sb", [P, ROWS_N])
        bqk_sb = sb("bqk_sb", [P, 2])
        dl_sb = sb("dl_sb", [P, 1])
        lam = sb("lam", [P, 2])
        ids_sb = sb("ids_sb", [P, SEQS], U32)
        ids_now = sb("ids_now", [P, 2, U], U32)
        decq = sb("decq", [P, P])
        decqm = sb("decqm", [P, 2, P])
        deck = sb("deck", [P, P])
        causal = sb("causal", [P, P])
        ident = sb("ident", [P, P])
        tri = sb("tri", [P, P], BF16)
        ones_bf = sb("ones_bf", [P, P], BF16)
        par_i = sb("par_i", [P, 1], I32)
        rowno = sb("rowno", [P, 1], I32)
        par = sb("par", [P, 2])
        iota_e = sb("iota_e", [P, E])
        eoff = sb("eoff", [P, E])
        tokid = sb("tokid", [P, TOP, SEQS], I32)
        pad_rows = sb("pad_rows", [P, PADS, ROW])
        bias_bf = sb("bias_bf", [P, BIAS_N + 2 * D], BF16)
        selp = sb("selp", [P, E], BF16)
        sel = sb("sel", [P, E, P], BF16)
        eps_ln = sb("eps_ln", [P, 1])
        h2 = sb("h2", [P, SEQS, D])

        emb = sb("emb", [P, 2, U, D])
        h = sb("h", [P, 2, U, D])
        nm1 = sb("nm1", [P, U])
        nm2 = sb("nm2", [P, U])
        nm3 = sb("nm3", [P, U])
        st1 = sb("st1", [P, U, 6])
        mv1 = sb("mv1", [P, U, 2])
        ln1 = sb("ln1", [P, U])
        rs1 = sb("rs1", [P, U])
        xn = sb("xn", [P, U, D])
        xnT = sb("xnT", [P, W])
        relu_qk = sb("relu_qk", [P, 2, W])
        exp_qk = sb("exp_qk", [P, 2, W])
        qk = sb("qk", [P, 2, W])
        kd = sb("kd", [P, 2, W])
        qz = sb("qz", [P, U, 4, 2, P])
        qd = sb("qd", [P, W])
        vx = sb("vx", [P, 2, U, HEADS, VC])
        ndT = sb("ndT", [P, 2 * U * P])
        sm = sb("sm", [P, 4, U * 2, P])
        eb3 = sm[:, 0:2, :, :].rearrange("p b c d -> p (b c d)")[:, 0:BIAS_N + 2 * D]
        ebm = sm[:, 2:4, :, :].rearrange("p b c d -> p (b c d)")[:, 0:(BIAS_N + 2 * D) // 2].bitcast(BF16)
        den = sb("den", [P, U * HEADS])
        rec = sb("rec", [P, U * HEADS])
        o = sb("o", [P, U, D])
        oT = sb("oT", [P, W])
        aon = sb("aon", [P, U, D])
        hlb = sb("hlb", [P, 2, U, D])
        st2 = sb("st2", [P, U, 6])
        mv2 = sb("mv2", [P, U, 2])
        ln2 = sb("ln2", [P, U])
        rs2 = sb("rs2", [P, U])
        aog = sb("aog", [P, U, D])
        st3 = sb("st3", [P, U, 6])
        mv3 = sb("mv3", [P, U, 2])
        ln3 = sb("ln3", [P, U])
        rs3 = sb("rs3", [P, U])
        rr = sb("rr", [P, 2, TOP, U, ROW])
        x2T = sb("x2T", [P, W])
        lg = sb("lg", [P, U, E])
        mx = sb("mx", [P, U, 8])
        mi = sb("mi", [P, U, 8], U32)
        mif = sb("mif", [P, U, TOP])
        ls = sb("ls", [P, U, E + TOP])
        es = sb("es", [P, U, E + TOP])
        ssum = sb("ssum", [P, U])
        rsum = sb("rsum", [P, U])
        mk = sb("mk", [P, TOP, U, E])
        msum = sb("msum", [P, U, E], BF16)
        cum = sb("cum", [P, 2, E], BF16)
        mpair = sb("mpair", [P, E], BF16)
        rank = sb("rank", [P, U, E])
        slotp = sb("slotp", [P, TOP, U, E])
        slotf = sb("slotf", [P, TOP, U])
        slot = sb("slot", [P, 2, TOP, U], U32)

        cnt = sb("cnt", [P, E])
        cnt_i = sb("cnt_i", [P, E], I32)
        nt_i = sb("nt_i", [P, E], I32)
        ntf = sb("ntf", [P, E])
        onesf = sb("onesf", [P, E])
        endt = sb("endt", [P, E])
        tileno = sb("tileno", [P, 1])
        passed = sb("passed", [P, 2, E])
        tab = sb("tab", [P, 4])
        tile_row = sb("tile_row", [P, 1])
        pad_e = sb("pad_e", [P, 1])
        pad_lane = sb("pad_lane", [P, 1])
        pad_i = sb("pad_i", [P, 2], I32)
        padsel = sb("padsel", [P, E])
        padown = sb("padown", [P, E])
        padown_n = sb("padown_n", [P, 1])
        pad_piece = sb("pad_piece", [P, 1])
        padidx = sb("padidx", [P, 1], U32)
        tab_e = sb("tab_e", [1, TILES + 2], I32)
        tab_b = sb("tab_b", [1, TILES], I32)

        R = 8
        widx = sb("widx", [P, R, 2])
        pad_flat = pad_rows[:].rearrange("p a d -> p (a d)")
        n = [0]

        def in_pads(a, d):
            size = a * d
            n[0] += size
            return pad_flat[:, n[0] - size:n[0]].rearrange("p (a d) -> p a d", a=a)

        xs = in_pads(R, ROW)
        xT = in_pads(R, P)
        sg = in_pads(2, FF)
        hh = in_pads(2, FF)
        hT = in_pads(2, FF)
        ysb = rr[:].rearrange("p b k s r -> p (b k s r)")[:, 0:R * D].rearrange("p (r d) -> p r d", d=D)
        CB = 4
        ya = wgu_sb[:, 0:SEQS * D].rearrange("p (t d) -> p t d", d=D)
        yb = wgu_sb[:, SEQS * D:2 * SEQS * D].rearrange("p (t d) -> p t d", d=D)

        bank = [ps(f"bank{i}", [P, 512]) for i in range(8)]
        sc_ps = bank[0:4]
        xnT_ps = bank[4][:, 0:W]
        v_ps = bank[4][:, W:2 * W]
        qk_ps = bank[5]
        ndT_ps = bank[6].rearrange("p (q s l) -> p q s l", q=2, s=U)
        nd_ps = bank[6].rearrange("p (a f) -> p a f", f=VC)
        oT_ps = bank[6][:, 0:W]
        ao_ps = bank[6][:, W:2 * W]
        x2T_ps = bank[7][:, 0:W]
        lg_ps = bank[7][:, W:W + U * E]
        rk_ps = bank[7][:, W + U * E:W + 2 * U * E]
        cnt_ps = bank[7][:, W + 2 * U * E:W + 2 * U * E + E]
        tab_ps = bank[5]
        gu_ps = [bank[0], bank[1]]
        hT_ps = [bank[2][:, 0:FF], bank[3][:, 0:FF]]
        xT_ps = [bank[4][:, 0:P], bank[5][:, 0:P]]
        y_ps = [bank[6][:, 0:D], bank[7][:, 0:D]]

        ids_in = sem("ids_in")
        small_in = sem("small_in")
        ebias_in = sem("ebias_in")
        experts_in = sem("experts_in")
        pool_const = sem("pool_const")
        dve_const = sem("dve_const")
        act_const = sem("act_const")
        bias_ready = sem("bias_ready")
        expert_bias_ready = sem("expert_bias_ready")
        sel_ready = sem("sel_ready")
        ids_staged_first = sem("ids_staged_first")
        ids_staged = [sem(f"ids_staged{b}") for b in range(2)]
        emb_in = [[sem(f"emb_in{b}{s}") for s in range(U)] for b in range(2)]
        emb_sum = sem("emb_sum")
        hlb_ready = sem("hlb_ready")
        h_ready = sem("h_ready")
        nm1_ready = sem("nm1_ready")
        nm2_ready = sem("nm2_ready")
        nm3_ready = sem("nm3_ready")
        kd_ready = sem("kd_ready")
        qd_ready = sem("qd_ready")
        qeo_ready = sem("qeo_ready")
        qz_ready = sem("qz_ready")
        den_ready = sem("den_ready")
        o_ready = sem("o_ready")
        oT_made = sem("oT_made")
        aon_ready = sem("aon_ready")
        st1_ready = sem("st1_ready")
        mv1_ready = sem("mv1_ready")
        ln1_ready = sem("ln1_ready")
        rs1_ready = sem("rs1_ready")
        xn_ready = sem("xn_ready")
        xnT_made = sem("xnT_made")
        xnT_ready = sem("xnT_ready")
        qk_made = sem("qk_made")
        v_made = sem("v_made")
        act_qk = sem("act_qk")
        qk_ready = sem("qk_ready")
        v_ready = sem("v_ready")
        sc_made = sem("sc_made")
        sm_ready = sem("sm_ready")
        nd_made = sem("nd_made")
        ndT_ready = sem("ndT_ready")
        ndtok_made = sem("ndtok_made")
        rec_ready = sem("rec_ready")
        oT_ready = sem("oT_ready")
        ao_made = sem("ao_made")
        st2_ready = sem("st2_ready")
        mv2_ready = sem("mv2_ready")
        ln2_ready = sem("ln2_ready")
        rs2_ready = sem("rs2_ready")
        aog_ready = sem("aog_ready")
        h2_ready = sem("h2_ready")
        st3_ready = sem("st3_ready")
        mv3_ready = sem("mv3_ready")
        ln3_ready = sem("ln3_ready")
        rs3_ready = sem("rs3_ready")
        rr0_ready = sem("rr0_ready")
        rr1_ready = [sem(f"rr1_ready{b}") for b in range(2)]
        x2T_made = sem("x2T_made")
        x2T_ready = sem("x2T_ready")
        lg_made = sem("lg_made")
        lg_ready = sem("lg_ready")
        mx_ready = sem("mx_ready")
        mi_ready = sem("mi_ready")
        mif_ready = sem("mif_ready")
        ls_ready = sem("ls_ready")
        es_ready = sem("es_ready")
        ssum_ready = sem("ssum_ready")
        rsum_ready = sem("rsum_ready")
        w_ready = [sem(f"w_ready{b}") for b in range(2)]
        mk_ready = sem("mk_ready")
        msum_ready = sem("msum_ready")
        mpair_ready = sem("mpair_ready")
        cum_ready = sem("cum_ready")
        rk_made = sem("rk_made")
        rank_ready = sem("rank_ready")
        slotp_ready = sem("slotp_ready")
        slotf_ready = sem("slotf_ready")
        slot_ready = [sem(f"slot_ready{b}") for b in range(2)]
        rows_out = [[sem(f"rows_out{b}{c}") for c in range(TOP * U)] for b in range(2)]
        cnt_made = sem("cnt_made")
        tab_step = sem("tab_step")
        tab_made = sem("tab_made")
        tab_ready = sem("tab_ready")
        pads_out = sem("pads_out")
        padidx_ready = sem("padidx_ready")
        pads_made = sem("pads_made")
        xs_in = [sem(f"xs_in{r}") for r in range(R)]
        widx_ready = sem("widx_ready")
        xT_made = sem("xT_made")
        xT_ready = sem("xT_ready")
        gu_made = sem("gu_made")
        sg_ready = sem("sg_ready")
        hh_ready = sem("hh_ready")
        hT_made = sem("hT_made")
        hT_ready = sem("hT_ready")
        y_made = sem("y_made")
        y_ready = [sem(f"y_ready{r}") for r in range(R)]
        y_out = [sem(f"y_out{r}") for r in range(R)]
        ya_in = [sem(f"ya_in{c}") for c in range(SEQS // CB)]
        yb_in = [sem(f"yb_in{c}") for c in range(SEQS // CB)]
        sum1_ready = sem("sum1_ready")
        sum_ready = sem("sum_ready")
        stored = sem("stored")

        CONST_POOL = 17
        TAB_STEPS = 14

        block = ctx.enter_context(nc.Block())

        def lap(t, q):
            return t + (q // R + 1)

        def stands_first(eng, passed):
            eng.wait_ge(passed, 1)

        def steps(eng, step, first, last):
            n = (last - first) // 2
            if n > 1:
                with eng.Fori(0, n) as t:
                    for k in range(2):
                        step(t * 2 + (first + k), (first + k) % 2)
            else:
                n = 0
            for i in range(first + 2 * n, last):
                step(i, i % 2)

        def skewed(eng, step):
            step(-1, 1, True, False, False, False, False)
            step(0, 0, True, True, False, False, False)
            step(1, 1, True, True, True, False, False)
            step(2, 0, True, True, True, True, False)
            step(3, 1, True, True, True, True, True)
            steps(eng, lambda i, b: step(i, b, True, True, True, True, True), 4, UNITS - 1)
            step(UNITS - 1, (UNITS - 1) % 2, False, True, True, True, True)
            step(UNITS, UNITS % 2, False, False, True, True, True)
            step(UNITS + 1, (UNITS + 1) % 2, False, False, False, True, True)
            step(UNITS + 2, UNITS % 2, False, False, False, False, True)

        @block.sync
        def _(sp):
            sp.dma_start(ids_sb[:], ids).then_inc(ids_in, 16)
            sp.dma_start(rows_sb[:], rows.rearrange("(a n) -> a n", a=1).broadcast_to([P, ROWS_N])).then_inc(small_in, 16)
            sp.dma_start(bqk_sb[:], bqk).then_inc(small_in, 16)
            sp.dma_start(dl_sb[:], decay).then_inc(small_in, 16)
            sp.dma_start(wqkv_sb[:], wqkv).then_inc(small_in, 16)
            sp.dma_start(wout_sb[:], wout).then_inc(small_in, 16)
            sp.dma_start(wgate_sb[:], wgate).then_inc(small_in, 16)
            for c in range(3):
                sp.dma_start(eb3[32 * c:32 * c + 32, :], ebias).then_inc(ebias_in, 16)
            for c in range(8):
                sp.wait_ge(h_ready, c + 1)
                n = E * 2 * FF // 8
                sp.dma_start(wgu_sb[:, c * n:(c + 1) * n], wgu[:, c * n:(c + 1) * n]).then_inc(experts_in, 16)
            for c in range(4):
                sp.wait_ge(h_ready, c + 9)
                n = E * 2 * D // 4
                sp.dma_start(wd_sb[:, c * n:(c + 1) * n], wd[:, c * n:(c + 1) * n]).then_inc(experts_in, 16)

            def rows_complete():
                for b in range(2):
                    for c in range(TOP * U):
                        sp.wait_ge(rows_out[b][c], 16 * (UNITS // 2))
                sp.wait_ge(pads_out, 16 * 2)

            sp.wait_ge(tab_ready, 2)

            def load_tiles(t, reused):
                _, first_rows = nc.values_load_multi_w_load_instructions(tab_b[0:1, bass.ds(t * R, R)], engines=(mybir.EngineType.SP,),
                                                  min_val=0, max_val=DUMMY,
                                                  skip_runtime_bounds_check_because="VectorE keeps them in 0 .. DUMMY")
                if not reused:
                    rows_complete()
                for r, row in enumerate(first_rows):
                    if reused:
                        sp.wait_ge(xT_made, t * R + (r + 1 - R))
                        sp.wait_ge(widx_ready, t * R + (r + 1 - R))
                    sp.dma_start(xs[:, r, :], xs_dram[bass.ds(row, P), :]).then_inc(xs_in[r], 16)

            load_tiles(0, False)
            with sp.Fori(1, TILES // R) as t:
                load_tiles(t, True)

            for r in range(R):
                sp.wait_ge(y_out[r], 16 * (TILES // R))

            y_t = y_dram.rearrange("(k p t) d -> p k t d", k=TOP, p=P)

            sp.wait_ge(gu_made, TILES)
            for c in range(SEQS // CB):
                for k, (dst, arrived) in enumerate(((ya, ya_in), (yb, yb_in))):
                    sp.dma_start(dst[:, c * CB:(c + 1) * CB, :], y_t[:, k, c * CB:(c + 1) * CB, :]).then_inc(arrived[c], 16)
            sp.wait_ge(stored, 16 * (SEQS // CB))

        @block.gpsimd
        def _(pool):
            pool.wait_ge(ids_in, 16)

            def gather(u, b, staged, count):
                pool.tensor_copy(ids_now[:, b, :], ids_sb[:, bass.ds(u * U, U)]).then_inc(staged, 1)
                stands_first(pool, ids_in)
                pool.wait_ge(staged, count)
                for s in range(U):
                    pool.indirect_dma_start(emb[:, b, s, :], None, wt,
                                            bass.IndirectOffsetOnAxis(ap=ids_now[:, b, s:s + 1], axis=0))\
                        .then_inc(emb_in[b][s], 16)

            def add_b(b, arrived):
                for s in range(U):
                    pool.wait_ge(emb_in[b][s], 16 * arrived)
                pool.tensor_tensor(emb[:, b, :, :], emb[:, b, :, :],
                                   rows_sb[:, None, ROW_TOKB:ROW_TOKB + D].broadcast_to([P, U, D]), ALU.add).then_inc(emb_sum, 1)

            def add_lnb(i, b):
                pool.wait_ge(h_ready, i)
                if not isinstance(i, int) or i >= 3:
                    pool.wait_ge(h2_ready, i - 2)
                pool.tensor_tensor(hlb[:, b, :, :], h[:, b, :, :],
                                   rows_sb[:, None, ROW_LNB:ROW_LNB + D].broadcast_to([P, U, D]), ALU.add).then_inc(hlb_ready, 1)

            def keys(i, b):
                stands_first(pool, pool_const)
                pool.wait_ge(qk_ready, i + 1)
                if not isinstance(i, int) or i >= 2:
                    pool.wait_ge(sc_made, 4 * i - 4)
                pool.tensor_tensor(kd[:, b, :].rearrange("p (s l) -> p s l", l=P),
                                   qk[:, 1, :].rearrange("p (s l) -> p s l", l=P),
                                   deck[:, None, :].broadcast_to([P, U, P]), ALU.mult).then_inc(kd_ready, 1)

            def scatter(b, count):
                stands_first(pool, pool_const)
                pool.wait_ge(slot_ready[b], count)
                pool.wait_ge(w_ready[b], count)
                pool.wait_ge(rr1_ready[b], count)
                for k in range(TOP):
                    for s in range(U):
                        pool.indirect_dma_start(xs_dram, bass.IndirectOffsetOnAxis(ap=slot[:, b, k, s:s + 1], axis=0),
                                                rr[:, b, k, s, :], None).then_inc(rows_out[b][k * U + s], 16)

            def gather_static(u):
                if u <= 4:
                    gather(u, u % 2, ids_staged_first, u + 1)
                else:
                    gather(u, u % 2, ids_staged[u % 2], (u - 3) // 2)

            def step(i):
                if i + 2 < UNITS:
                    pool.wait_ge(h_ready, i + 1)
                    gather_static(i + 2)
                if i < UNITS:
                    keys(i, i % 2)
                    add_lnb(i + 1, i % 2)
                if i + 2 < UNITS:
                    add_b(i % 2, (i + 2) // 2 + 1)
                if i >= 3:
                    scatter((i - 3) % 2, (i - 3) // 2 + 1)

            gather_static(0)
            gather_static(1)

            n = [0]

            def made(ins):
                n[0] += 1
                ins.then_inc(pool_const, 1)

            made(pool.memset(ident[:], 0.0))
            made(pool.memset(causal[:], 1.0))
            made(pool.memset(tri[:], 1.0))
            made(pool.memset(ones_bf[:], 1.0))
            made(pool.iota(rowno[:], [[0, 1]], base=0, channel_multiplier=1))
            made(pool.memset(selp[:], 0.0))
            made(pool.iota(par_i[:], [[0, 1]], base=0, channel_multiplier=1))
            made(pool.iota(tokid[:], [[TOK, TOP], [1, SEQS]], base=0, channel_multiplier=SEQS))
            made(pool.iota(iota_e[:], [[1, E]], base=0, channel_multiplier=0, allow_small_or_imprecise_dtypes=True))
            made(pool.iota(eoff[:], [[REG, E]], base=0, channel_multiplier=0, allow_small_or_imprecise_dtypes=True))
            made(pool.iota(tileno[:], [[0, 1]], base=0, channel_multiplier=1, allow_small_or_imprecise_dtypes=True))
            pool.wait_ge(small_in, 16 * 6)
            add_b(0, 1)
            pool.wait_ge(pool_const, n[0])
            made(pool.affine_select(out=ident[:], in_=ident[:], compare_op=NOT_EQUAL, fill=1.0, base=0,
                                    pattern=[[-1, P]], channel_multiplier=1))
            made(pool.affine_select(out=causal[:], in_=causal[:], compare_op=ALU.is_ge, fill=0.0, base=0,
                                    pattern=[[1, P]], channel_multiplier=-1))
            made(pool.affine_select(out=tri[:], in_=tri[:], compare_op=ALU.is_gt, fill=0.0, base=0,
                                    pattern=[[1, P]], channel_multiplier=-1))
            for c in range(3):
                made(pool.affine_select(out=selp[:], in_=selp[:], compare_op=NOT_EQUAL, fill=1.0, base=-32 * c,
                                        pattern=[[-1, E]], channel_multiplier=1))
                pool.wait_ge(pool_const, n[0])
            assert n[0] == CONST_POOL

            add_b(1, 1)
            pool.memset(pad_rows[:], 0.0).then_inc(pads_made, 1)
            pool.wait_ge(pads_made, 1)
            pool.iota(pad_rows[:, :, ROW - 1].bitcast(I32), [[0, PADS]], base=SKIP, channel_multiplier=0).then_inc(pads_made, 1)
            for i in range(5):
                step(i)
            pool.wait_ge(pads_made, 2)
            pool.dma_start(xs_dram[DUMMY:DUMMY + P, :], pad_rows[:, 0, :]).then_inc(pads_out, 16)
            with pool.Fori(2, UNITS // 2 - 2) as t:
                for b in (1, 0):
                    i = t * 2 + (2 - b)
                    pool.wait_ge(h_ready, i + 1)
                    gather(i + 2, b, ids_staged[b], t)
                    keys(i, b)
                    add_lnb(i + 1, b)
                    add_b(b, t + (3 - b))
                    scatter(1 - b, t)
            for i in range(UNITS - 3, UNITS + 2):
                step(i)

            pool.wait_ge(padidx_ready, 1)
            pool.indirect_dma_start(xs_dram.rearrange("n (a d) -> (n a) d", a=PIECES),
                                    bass.IndirectOffsetOnAxis(ap=padidx[:, 0:1], axis=0),
                                    pad_rows[:].rearrange("p a d -> p (a d)"), None).then_inc(pads_out, 16)
            step(UNITS + 2)

            with pool.Fori(1, TILES // R + 1) as t:
                for r in range(R):
                    stands_first(pool, pool_const)
                    pool.wait_ge(y_ready[r], t)
                    pool.indirect_dma_start(y_dram, bass.IndirectOffsetOnAxis(ap=widx[:, r, 1:2].bitcast(U32), axis=0),
                                            ysb[:, r, :], None, bounds_check=TOP * TOK - 1, oob_is_err=False)\
                        .then_inc(y_out[r], 16)

        @block.scalar
        def _(act):
            nc.scalar.preload_act_table_set("natural_log_exp_and_others")
            act.wait_ge(small_in, 16 * 6)
            nc.scalar.activation(lam[:, 0:1], dl_sb[:], ACT.Exp, scale=-1.0).then_inc(act_const, 1)
            act.wait_ge(dve_const, 1)

            def rstd(var, ln, rs, mv_ready, ln_ready, rs_ready, u):
                act.wait_ge(mv_ready, u + 1)
                nc.scalar.activation(ln[:], var[:, :, 1], ACT.Ln, bias=eps_ln[:, 0:1]).then_inc(ln_ready, 1)
                act.wait_ge(ln_ready, u + 1)
                nc.scalar.activation(rs[:], ln[:], ACT.Exp, scale=-0.5).then_inc(rs_ready, 1)

            def make_h(u, b):
                act.wait_ge(emb_sum, u + 1)
                if later(u, 2):
                    act.wait_ge(hlb_ready, u - 1)
                nc.scalar.activation(h[:, b, :, :], emb[:, b, :, :], ACT.Copy, scale=EMB_SCALE).then_inc(h_ready, 1)

            def later(i, k):
                return not isinstance(i, int) or i >= k

            def step(i, b, norm, first, second, third, fourth):
                c = 1 - b
                if norm:
                    make_h(i + 1, c)
                if third:
                    rstd(mv2, ln2, rs2, mv2_ready, ln2_ready, rs2_ready, i - 2)
                    act.wait_ge(nm2_ready, i - 1)
                    if later(i, 3):
                        act.wait_ge(aog_ready, i - 2)
                    for s in range(U):
                        ins = nc.scalar.activation(aon[:, s, :], ao_ps[:, s * D:(s + 1) * D], ACT.Identity,
                                                   bias=nm2[:, s:s + 1], scale=rs2[:, s:s + 1])
                    ins.then_inc(aon_ready, 1)
                if first:
                    act.wait_ge(qk_made, i + 1)
                    if later(i, 1):
                        act.wait_ge(qk_ready, i)
                    for q in range(2):
                        nc.scalar.activation(relu_qk[:, q, :], qk_ps[:, q * W:(q + 1) * W], ACT.Relu,
                                             bias=bqk_sb[:, q:q + 1]).then_inc(act_qk, 1)
                        nc.scalar.activation(exp_qk[:, q, :], qk_ps[:, q * W:(q + 1) * W], ACT.Exp,
                                             bias=bqk_sb[:, q:q + 1]).then_inc(act_qk, 1)
                    act.wait_ge(v_made, i + 1)
                    if later(i, 2):
                        act.wait_ge(nd_made, i - 1)
                    for s in range(U):
                        ins = nc.scalar.activation(vx[:, b, s, :, 0:HD],
                                                   v_ps[:, s * D:(s + 1) * D].rearrange("p (a f) -> p a f", f=HD), ACT.Copy)
                    ins.then_inc(v_ready, 1)
                if second:
                    act.wait_ge(nd_made, i)
                    nc.scalar.activation(ndT[:], bank[6][:], ACT.Copy).then_inc(ndT_ready, 1)
                if third:
                    rstd(mv3, ln3, rs3, mv3_ready, ln3_ready, rs3_ready, i - 2)
                    act.wait_ge(nm3_ready, i - 1)
                    if later(i, 4):
                        for q in range(TOP * U):
                            if b == 0:
                                act.wait_ge(rows_out[b][q], 8 * i - 16)
                            else:
                                act.wait_ge(rows_out[b][q], 8 * i - 24)
                    for s in range(U):
                        ins = nc.scalar.activation(rr[:, b, 0, s, 0:D],
                                                   h2[:, bass.ds(i * U + (s - 2 * U), 1), :].rearrange("p a d -> p (a d)"),
                                                   ACT.Identity, bias=nm3[:, s:s + 1], scale=rs3[:, s:s + 1])
                    ins.then_inc(rr0_ready, 1)
                if norm:
                    rstd(mv1, ln1, rs1, mv1_ready, ln1_ready, rs1_ready, i + 1)
                if third:
                    act.wait_ge(x2T_made, i - 1)
                    nc.scalar.activation(x2T[:], x2T_ps, ACT.Copy).then_inc(x2T_ready, 1)
                if norm:
                    act.wait_ge(nm1_ready, i + 2)
                    if later(i, 0):
                        act.wait_ge(xnT_made, i + 1)
                    for s in range(U):
                        ins = nc.scalar.activation(xn[:, s, :], h[:, c, s, :], ACT.Identity, bias=nm1[:, s:s + 1],
                                                   scale=rs1[:, s:s + 1])
                    ins.then_inc(xn_ready, 1)
                if second:
                    act.wait_ge(oT_made, i)
                    nc.scalar.activation(oT[:], oT_ps, ACT.Copy).then_inc(oT_ready, 1)
                if norm:
                    act.wait_ge(xnT_made, i + 2)
                    nc.scalar.activation(xnT[:], xnT_ps, ACT.Copy).then_inc(xnT_ready, 1)
                if first:
                    act.wait_ge(qd_ready, i + 1)
                    if later(i, 1):
                        act.wait_ge(sc_made, 4 * i)
                    for g in range(2, 4):
                        rows_g = slice(32 * g, 32 * g + 32)
                        for q in range(2):
                            ins = nc.scalar.activation(qz[rows_g, :, g, q, :], qd[rows_g, :].rearrange("p (s l) -> p s l", l=P),
                                                       ACT.Copy, scale=par[rows_g, q:q + 1])
                    ins.then_inc(qeo_ready, 1)
                if third:
                    act.wait_ge(ls_ready, 2 * i - 2)
                    nc.scalar.activation(es[:], ls[:], ACT.Exp).then_inc(es_ready, 1)
                    act.wait_ge(rr0_ready, i - 1)
                    nc.scalar.activation(rr[:, b, 1, :, 0:D], rr[:, b, 0, :, 0:D], ACT.Copy).then_inc(rr1_ready[b], 1)

            skewed(act, step)

            act.wait_ge(pool_const, CONST_POOL)
            nc.scalar.activation(sel[:], selp[:, :, None].broadcast_to([P, E, P]), ACT.Copy).then_inc(sel_ready, 1)
            nc.scalar.preload_act_table(ACT.Silu)

            def evac_xT(j, r):
                act.wait_ge(xT_made, j + 1)
                if not isinstance(j, int) or j >= R:
                    act.wait_ge(gu_made, j - (R - 1))
                nc.scalar.activation(xT[:, r % R, :], xT_ps[r % 2], ACT.Copy).then_inc(xT_ready, 1)

            def silu(j, r):
                act.wait_ge(gu_made, j + 1)
                if not isinstance(j, int) or j >= 2:
                    act.wait_ge(hh_ready, j - 1)
                nc.scalar.activation(sg[:, r % 2, :], gu_ps[r % 2][:, 0:FF], ACT.Silu).then_inc(sg_ready, 1)

            evac_xT(0, 0)
            with act.Fori(0, TILES // R - 1) as t:
                for r in range(R):
                    evac_xT_j = t * R + (r + 1)
                    act.wait_ge(xT_made, evac_xT_j + 1)
                    nc.scalar.activation(xT[:, (r + 1) % R, :], xT_ps[(r + 1) % 2], ACT.Copy).then_inc(xT_ready, 1)
                    act.wait_ge(gu_made, t * R + (r + 1))
                    nc.scalar.activation(sg[:, r % 2, :], gu_ps[r % 2][:, 0:FF], ACT.Silu).then_inc(sg_ready, 1)
            for j in range(TILES - R, TILES):
                if j + 1 < TILES:
                    evac_xT(j + 1, j + 1)
                silu(j, j)

            out_t = out.rearrange("(t p) d -> p t d", p=P)
            for c in range(SEQS // CB):
                act.wait_ge(sum_ready, c + 1)
                act.dma_start(out_t[:, c * CB:(c + 1) * CB, :], yb[:, c * CB:(c + 1) * CB, :]).then_inc(stored, 16)

        @block.vector
        def _(dve):
            V = nc.vector
            n = [0]

            def link(ins):
                n[0] += 1
                ins.then_inc(dve_const, 1)
                dve.wait_ge(dve_const, n[0])

            V.memset(eps_ln[:], LN_EPS)
            V.memset(tab_e[:], 0)
            V.memset(vx[:], 0.0)
            V.memset(qz[:], 0.0)
            V.memset(decq[:, 0:1], 1.0)
            link(V.memset(bias_bf[:], 0.0))
            V.memset(vx[:, :, :, :, HD], 1.0)

            def split(cols):
                q = slice(0, 96)
                link(V.tensor_copy(ebm[q, cols], eb3[q, cols]))
                V.tensor_copy(bias_bf[0:32, cols], ebm[0:32, cols])
                link(V.tensor_tensor(eb3[q, cols], eb3[q, cols], ebm[q, cols], ALU.subtract))
                link(V.tensor_copy(ebm[q, cols], eb3[q, cols]))
                V.tensor_copy(bias_bf[32:64, cols], ebm[32:64, cols])
                link(V.tensor_tensor(eb3[q, cols], eb3[q, cols], ebm[q, cols], ALU.subtract))
                link(V.tensor_copy(bias_bf[64:96, cols], eb3[64:96, cols]))

            def powers():
                dve.wait_ge(act_const, 1)
                link(V.tensor_scalar_add(lam[:, 0:1], lam[:, 0:1], 1.0))
                link(V.reciprocal(lam[:, 1:2], lam[:, 0:1]))
                link(V.tensor_scalar(lam[:, 0:1], lam[:, 1:2], 0.01, 0.99, ALU.mult, ALU.add))
                for c in range(7):
                    m = 1 << c
                    link(V.tensor_scalar(decq[:, m:2 * m], decq[:, 0:m], lam[:, c % 2:c % 2 + 1], None, ALU.mult))
                    link(V.tensor_tensor(lam[:, (c + 1) % 2:(c + 1) % 2 + 1], lam[:, c % 2:c % 2 + 1],
                                         lam[:, c % 2:c % 2 + 1], ALU.mult))

            def bias_and_decays():
                dve.wait_ge(ebias_in, 48)
                split(slice(BIAS_N, BIAS_N + 2 * D))
                V.memset(cum[:, 1, :], 0.0).then_inc(bias_ready, 1)
                link(V.reciprocal(deck[:], decq[:]))
                dve.wait_ge(pool_const, CONST_POOL)
                link(V.tensor_scalar(par_i[:], par_i[:], 4, 1, ALU.logical_shift_right, ALU.bitwise_and))
                link(V.tensor_copy(par[:, 1:2], par_i[:]))
                link(V.tensor_scalar(par[:, 0:1], par[:, 1:2], -1.0, 1.0, ALU.mult, ALU.add))
                link(V.tensor_scalar_mul(decq[:], decq[:], 1.0 / float(HD) ** 0.5))
                for q in range(2):
                    link(V.tensor_scalar(decqm[:, q, :], decq[:], par[:, q:q + 1], None, ALU.mult))

            powers()

            def late_setup():
                split(slice(0, BIAS_N))
                V.memset(onesf[:], 1.0).then_inc(expert_bias_ready, 1)
                link(V.tensor_scalar(pad_i[:, 0:1], rowno[:], PAD_LANES.bit_length() - 1, None, ALU.logical_shift_right))
                link(V.tensor_scalar(pad_i[:, 1:2], rowno[:], PAD_LANES - 1, None, ALU.bitwise_and))
                link(V.tensor_copy(pad_e[:], pad_i[:, 0:1]))
                link(V.tensor_copy(pad_lane[:], pad_i[:, 1:2]))
                link(V.tensor_scalar(padsel[:], iota_e[:], pad_e[:, 0:1], None, ALU.is_equal))
                link(V.tensor_scalar_mul(pad_lane[:], pad_lane[:], float(PADS * PIECES)))
                link(V.scalar_tensor_tensor(out=pad_piece[:], in0=pad_e[:], scalar=float(REG * PIECES), in1=pad_lane[:],
                                            op0=ALU.mult, op1=ALU.add))
                link(V.tensor_scalar_mul(tile_row[:], tileno[:], float(P)))

            lng = rows_sb[:, None, ROW_LNG:ROW_LNG + D].broadcast_to([P, U, D])
            bgate = rows_sb[:, None, ROW_BGATE:ROW_BGATE + E].broadcast_to([P, U, E])

            def stats(src, st, mv, st_ready, mv_ready, u):
                for s in range(U):
                    ins = V.bn_stats(st[:, s, :], src(s))
                ins.then_inc(st_ready, 1)
                stands_first(dve, dve_const)
                dve.wait_ge(st_ready, u)
                for s in range(U):
                    ins = V.bn_aggr(mv[:, s, :], st[:, s, :])
                ins.then_inc(mv_ready, 1)

            def later(i, k):
                return not isinstance(i, int) or i >= k

            def negmean(nm, mv, rs, rs_ready, nm_ready, u):
                dve.wait_ge(rs_ready, u)
                V.scalar_tensor_tensor(out=nm[:], in0=mv[:, :, 0], scalar=-1.0, in1=rs[:], op0=ALU.mult,
                                       op1=ALU.mult).then_inc(nm_ready, 1)

            def step(i, b, norm, first, second, third, fourth):
                c = 1 - b
                if isinstance(i, int) and i == 0:
                    bias_and_decays()
                if isinstance(i, int) and i == 1:
                    late_setup()
                if third:
                    negmean(nm2, mv2, rs2, rs2_ready, nm2_ready, i - 1)
                if second:
                    mask(0, i - 1)
                    mask(1, i - 1)
                if norm:
                    dve.wait_ge(h_ready, i + 2)
                    stats(lambda s: h[:, c, s, :], st1, mv1, st1_ready, mv1_ready, i + 2)
                if third:
                    dve.wait_ge(aon_ready, i - 1)
                    V.tensor_tensor(aog[:], aon[:], lng, ALU.mult).then_inc(aog_ready, 1)
                if second:
                    mask(2, i - 1)
                if third:
                    dve.wait_ge(aog_ready, i - 1)
                    dve.wait_ge(hlb_ready, i - 1)
                    V.tensor_tensor(h2[:, bass.ds(i * U - 2 * U, U), :], aog[:], hlb[:, b, :, :], ALU.add).then_inc(h2_ready, 1)
                if second:
                    mask(3, i - 1)
                if third:
                    stands_first(dve, dve_const)
                    dve.wait_ge(h2_ready, i - 1)
                    stats(lambda s: h2[:, bass.ds(i * U + (s - 2 * U), 1), :].rearrange("p a d -> p (a d)"),
                          st3, mv3, st3_ready, mv3_ready, i - 1)
                if first:
                    if later(i, 1):
                        dve.wait_ge(kd_ready, i)
                    dve.wait_ge(act_qk, 4 * i + 4)
                    V.scalar_tensor_tensor(out=qk[:], in0=exp_qk[:], scalar=1.0, in1=relu_qk[:],
                                           op0=ALU.min, op1=ALU.add).then_inc(qk_ready, 1)
                if third:
                    negmean(nm3, mv3, rs3, rs3_ready, nm3_ready, i - 1)
                if second:
                    dve.wait_ge(ndtok_made, i)
                    V.tensor_scalar_add(den[:], nd_ps[:, :, HD], DEN_EPS).then_inc(den_ready, 1)
                if fourth:
                    dve.wait_ge(es_ready, i - 2)
                    V.tensor_reduce(ssum[:], es[:, :, 0:E], AXX, ALU.add).then_inc(ssum_ready, 1)
                if second:
                    dve.wait_ge(den_ready, i)
                    V.reciprocal(rec[:], den[:]).then_inc(rec_ready, 1)
                if fourth:
                    dve.wait_ge(rk_made, i - 2)
                    V.tensor_tensor(rank[:], rk_ps.rearrange("p (s e) -> p s e", e=E),
                                    eoff[:, None, :].broadcast_to([P, U, E]), ALU.add).then_inc(rank_ready, 1)
                    dve.wait_ge(rr0_ready, i - 2)
                    V.tensor_copy(rr[:, c, :, :, D + 1].bitcast(I32), tokid[:, :, bass.ds(i * U - 3 * U, U)])
                    dve.wait_ge(ssum_ready, i - 2)
                    V.reciprocal(rsum[:], ssum[:]).then_inc(rsum_ready, 1)
                if norm:
                    negmean(nm1, mv1, rs1, rs1_ready, nm1_ready, i + 2)
                if second:
                    dve.wait_ge(rec_ready, i)
                    V.tensor_tensor(o[:].rearrange("p s (a f) -> p (s a) f", f=HD), nd_ps[:, :, 0:HD],
                                    rec[:, :, None].broadcast_to([P, U * HEADS, HD]), ALU.mult).then_inc(o_ready, 1)
                if first:
                    dve.wait_ge(qk_ready, i + 1)
                    if later(i, 1):
                        dve.wait_ge(qeo_ready, i)
                    hi = slice(P // 2, P)
                    V.tensor_tensor(qd[hi, :].rearrange("p (s l) -> p s l", l=P),
                                    qk[hi, 0, :].rearrange("p (s l) -> p s l", l=P),
                                    decq[hi, None, :].broadcast_to([P // 2, U, P]), ALU.mult).then_inc(qd_ready, 1)
                if fourth:
                    dve.wait_ge(rsum_ready, i - 2)
                    V.tensor_tensor(rr[:, c, :, :, D].rearrange("p k s -> p s k"), es[:, :, E:E + TOP],
                                    rsum[:, :, None].broadcast_to([P, U, TOP]), ALU.mult).then_inc(w_ready[c], 1)
                    V.tensor_tensor(mpair[:], msum[:, 0, :], msum[:, 1, :], ALU.add).then_inc(mpair_ready, 1)
                    dve.wait_ge(rank_ready, i - 2)
                    for k in range(TOP):
                        V.tensor_tensor(slotp[:, k, :, :], rank[:], mk[:, k, :, :], ALU.mult).then_inc(slotp_ready, 1)
                    dve.wait_ge(mpair_ready, i - 2)
                    V.tensor_tensor(cum[:, c, :], cum[:, b, :], mpair[:], ALU.add).then_inc(cum_ready, 1)
                if first:
                    if later(i, 1):
                        dve.wait_ge(sc_made, 4 * i)
                    query(0)
                    query(1)
                if fourth:
                    dve.wait_ge(slotp_ready, 2 * i - 4)
                    V.tensor_reduce(slotf[:], slotp[:], AXX, ALU.add).then_inc(slotf_ready, 1)
                    dve.wait_ge(slotf_ready, i - 2)
                    V.tensor_copy(slot[:, c, :, :], slotf[:]).then_inc(slot_ready[c], 1)
                if third:
                    dve.wait_ge(lg_made, i - 1)
                    V.tensor_tensor(lg[:], lg_ps.rearrange("p (s e) -> p s e", e=E), bgate, ALU.add).then_inc(lg_ready, 1)
                    stands_first(dve, dve_const)
                    dve.wait_ge(lg_ready, i - 1)
                    for s in range(U):
                        V.max(mx[:, s, :], lg[:, s, :]).then_inc(mx_ready, 1)
                    dve.wait_ge(mx_ready, 2 * i - 2)
                    m1 = mx[:, :, 0:1]
                    V.tensor_tensor(ls[:, :, 0:E], lg[:], m1.broadcast_to([P, U, E]), ALU.subtract).then_inc(ls_ready, 1)
                    V.tensor_tensor(ls[:, :, E:E + TOP], mx[:, :, 0:TOP], m1.broadcast_to([P, U, TOP]),
                                    ALU.subtract).then_inc(ls_ready, 1)
                    for s in range(U):
                        V.max_index(mi[:, s, :], mx[:, s, :], lg[:, s, :]).then_inc(mi_ready, 1)
                if second:
                    dve.wait_ge(ao_made, i)
                    stats(lambda s: ao_ps[:, s * D:(s + 1) * D], st2, mv2, st2_ready, mv2_ready, i)
                if third:
                    dve.wait_ge(mi_ready, 2 * i - 2)
                    V.tensor_copy(mif[:], mi[:, :, 0:TOP]).then_inc(mif_ready, 1)
                    dve.wait_ge(mif_ready, i - 1)
                    for k in range(TOP):
                        V.tensor_tensor(mk[:, k, :, :], iota_e[:, None, :].broadcast_to([P, U, E]),
                                        mif[:, :, k:k + 1].broadcast_to([P, U, E]), ALU.is_equal).then_inc(mk_ready, 1)
                    dve.wait_ge(mk_ready, 2 * i - 2)
                    V.tensor_tensor(msum[:], mk[:, 0, :, :], mk[:, 1, :, :], ALU.add).then_inc(msum_ready, 1)

            def query(g):
                rows_g = slice(32 * g, 32 * g + 32)
                V.tensor_tensor(qz[rows_g, :, g, :, :],
                                qk[rows_g, 0, :].rearrange("p (s q l) -> p s q l", q=1, l=P).broadcast_to([32, U, 2, P]),
                                decqm[rows_g, None, :, :].broadcast_to([32, U, 2, P]), ALU.mult).then_inc(qz_ready, 1)

            def mask(g, u):
                dve.wait_ge(sc_made, u * 4 + (g + 1))
                if later(u, 1):
                    dve.wait_ge(nd_made, u)
                V.tensor_tensor(sm[:, g, :, :], sc_ps[g][:].rearrange("p (a l) -> p a l", l=P),
                                causal[:, None, :].broadcast_to([P, 2 * U, P]), ALU.mult).then_inc(sm_ready, 1)

            skewed(dve, step)

            k = [0]

            def step_of(ins):
                k[0] += 1
                ins.then_inc(tab_step, 1)
                return k[0]

            def after(number):
                dve.wait_ge(tab_step, number)

            dve.wait_ge(cnt_made, 1)
            after(step_of(V.tensor_copy(cnt[:], cnt_ps)))
            own = step_of(V.tensor_tensor(padown[:], cnt[:], padsel[:], ALU.mult))
            rounded = step_of(V.tensor_scalar_add(cnt_i[:], cnt[:], float(P - 1)))
            after(own)
            own = step_of(V.tensor_reduce(padown_n[:], padown[:], AXX, ALU.add))
            after(rounded)
            shifted = step_of(V.tensor_scalar(nt_i[:], cnt_i[:], P.bit_length() - 1, None, ALU.logical_shift_right))
            after(own)
            V.scalar_tensor_tensor(out=padidx[:], in0=padown_n[:], scalar=float(PIECES), in1=pad_piece[:],
                                   op0=ALU.mult, op1=ALU.add).then_inc(padidx_ready, 1)
            after(shifted)
            after(step_of(V.tensor_copy(ntf[:], nt_i[:])))
            after(step_of(V.tensor_tensor_scan(endt[:], onesf[:], ntf[:], 0.0, ALU.mult, ALU.add)))
            after(step_of(V.tensor_scalar(passed[:, 0, :], endt[:], tileno[:, 0:1], None, ALU.is_le)))
            after(step_of(V.tensor_tensor(passed[:, 1, :], passed[:, 0, :], ntf[:], ALU.mult)))
            after(step_of(V.tensor_reduce(tab[:, 0:2], passed[:], AXX, ALU.add)))
            after(step_of(V.scalar_tensor_tensor(out=tab[:, 1:2], in0=tab[:, 1:2], scalar=-float(P), in1=tile_row[:],
                                                 op0=ALU.mult, op1=ALU.add)))
            after(step_of(V.scalar_tensor_tensor(out=tab[:, 1:2], in0=tab[:, 0:1], scalar=float(REG), in1=tab[:, 1:2],
                                                 op0=ALU.mult, op1=ALU.add)))
            step_of(V.tensor_scalar_min(tab[:, 0:1], tab[:, 0:1], float(E - 1)))
            step_of(V.tensor_scalar_min(tab[:, 1:2], tab[:, 1:2], float(DUMMY)))
            assert k[0] == TAB_STEPS
            dve.wait_ge(tab_made, 1)
            V.tensor_copy(tab_e[:, 2:TILES + 2], tab_ps[0:1, 0:TILES]).then_inc(tab_ready, 1)
            V.tensor_copy(tab_b[:], tab_ps[0:1, P:P + TILES]).then_inc(tab_ready, 1)

            def copy_widx(t, r):
                j = t * R + r
                dve.wait_ge(xs_in[r % R], lap(t, r) * 16)
                if later(j, R):
                    dve.wait_ge(y_out[r % R], lap(t, r) * 16 - 16)
                V.tensor_copy(widx[:, r % R, :], xs[:, r % R, D:D + 2]).then_inc(widx_ready, 1)

            def gate(t, r):
                j = t * R + r
                dve.wait_ge(sg_ready, j + 1)
                if later(j, 2):
                    dve.wait_ge(hT_made, j - 1)
                V.tensor_tensor(hh[:, r % 2, :], gu_ps[r % 2][:, FF:2 * FF], sg[:, r % 2, :], ALU.mult).then_inc(hh_ready, 1)

            def evac_hT(t, r):
                j = t * R + r
                dve.wait_ge(hT_made, j + 1)
                if later(j, 2):
                    dve.wait_ge(y_made, j - 1)
                V.tensor_copy(hT[:, r % 2, :], hT_ps[r % 2]).then_inc(hT_ready, 1)

            def evac_y(t, r):
                j = t * R + r
                dve.wait_ge(y_made, j + 1)
                V.tensor_scalar(ysb[:, r % R, :], y_ps[r % 2], widx[:, r % R, 0:1], None, ALU.mult).then_inc(y_ready[r % R], 1)

            def estep(t, r, full):
                if full or r + 1 < TILES:
                    copy_widx(t, r + 1)
                if full or r < TILES:
                    gate(t, r)
                if full or 0 <= r - 1 < TILES:
                    evac_hT(t, r - 1)
                if full or 0 <= r - 2 < TILES:
                    evac_y(t, r - 2)

            copy_widx(0, 0)
            for j in range(R):
                estep(0, j, False)
            with dve.Fori(1, TILES // R - 1) as t:
                for r in range(R):
                    estep(t, r, True)
            for j in range(TILES - R, TILES + 2):
                estep(0, j, False)

            for c in range(SEQS // CB):
                q = slice(c * CB, (c + 1) * CB)
                dve.wait_ge(ya_in[c], 16)
                dve.wait_ge(yb_in[c], 16)
                V.tensor_tensor(ya[:, q, :], ya[:, q, :], h2[:, q, :], ALU.add).then_inc(sum1_ready, 1)
                dve.wait_ge(sum1_ready, c + 1)
                V.tensor_tensor(yb[:, q, :], ya[:, q, :], yb[:, q, :], ALU.add).then_inc(sum_ready, 1)

        @block.tensor
        def _(pe):
            M = nc.tensor.matmul

            def later(i, k):
                return not isinstance(i, int) or i >= k

            pe.wait_ge(small_in, 16 * 6)
            pe.wait_ge(pool_const, CONST_POOL)

            def step(i, b, norm, first, second, third, fourth):
                c = 1 - b
                if second:
                    pe.wait_ge(kd_ready, i)
                    pe.wait_ge(qz_ready, 2 * i)
                    pe.wait_ge(qeo_ready, i)
                    if later(i, 2):
                        pe.wait_ge(sm_ready, 4 * i - 4)
                    for g in range(4):
                        for s in range(U):
                            ins = M(sc_ps[g][:, s * 2 * P:(s + 1) * 2 * P], kd[:, c, s * P:(s + 1) * P],
                                    qz[:, s, g, :, :].rearrange("p q l -> p (q l)"), start=True, stop=True)
                        ins.then_inc(sc_made, 1)
                if first:
                    if isinstance(i, int) and i == 0:
                        pe.wait_ge(bias_ready, 1)
                    pe.wait_ge(xnT_ready, i + 1)
                    for s in range(U):
                        M(v_ps[:, s * D:(s + 1) * D], xnT[:, s * P:(s + 1) * P], wqkv_sb[:, 2 * D:3 * D],
                          start=True, stop=False)
                        ins = M(v_ps[:, s * D:(s + 1) * D], ones_bf[0:96, :], bias_bf[0:96, BIAS_N:BIAS_N + D],
                                start=False, stop=True)
                    ins.then_inc(v_made, 1)
                if fourth:
                    pe.wait_ge(msum_ready, i - 2)
                    pe.wait_ge(lg_ready, i - 2)
                    if later(i, 4):
                        pe.wait_ge(cum_ready, i - 3)
                    M(rk_ps, tri[:], msum[:].rearrange("p s e -> p (s e)"), start=True, stop=False)
                    M(rk_ps.rearrange("p (s e) -> p s e", e=E), ones_bf[:], cum[:, b:b + 1, :].broadcast_to([P, U, E]), start=False, stop=False)
                    M(rk_ps[:, E:2 * E], ones_bf[:], msum[:, 0, :], start=False, stop=True).then_inc(rk_made, 1)
                if second:
                    pe.wait_ge(v_ready, i)
                    if later(i, 2):
                        pe.wait_ge(aon_ready, i - 1)
                    for g in range(4):
                        pe.wait_ge(sm_ready, 4 * i + (g - 3))
                        for s in range(U):
                            for q in range(2):
                                ins = M(ndT_ps[VC * g:VC * (g + 1), q, s, :], vx[:, c, s, 2 * g + q, :],
                                        sm[:, g, 2 * s + q, :], start=True, stop=True)
                    ins.then_inc(nd_made, 1)
                    pe.wait_ge(ndT_ready, i)
                    for s in range(U):
                        for q in range(2):
                            ins = nc.tensor.transpose(bank[6][:, (2 * s + q) * P:(2 * s + q + 1) * P],
                                                      ndT[:, (q * U + s) * P:(q * U + s + 1) * P], ident[:])
                    ins.then_inc(ndtok_made, 1)
                if third:
                    pe.wait_ge(rr0_ready, i - 1)
                    if later(i, 3):
                        pe.wait_ge(rank_ready, i - 2)
                    for s in range(U):
                        ins = nc.tensor.transpose(x2T_ps[:, s * P:(s + 1) * P], rr[:, b, 0, s, 0:D], ident[:])
                    ins.then_inc(x2T_made, 1)
                if second:
                    pe.wait_ge(o_ready, i)
                    for s in range(U):
                        ins = nc.tensor.transpose(oT_ps[:, s * P:(s + 1) * P], o[:, s, :], ident[:])
                    ins.then_inc(oT_made, 1)
                if third:
                    pe.wait_ge(x2T_ready, i - 1)
                    for s in range(U):
                        ins = M(lg_ps[:, s * E:(s + 1) * E], x2T[:, s * P:(s + 1) * P], wgate_sb[:], start=True, stop=True)
                    ins.then_inc(lg_made, 1)
                if norm:
                    pe.wait_ge(xn_ready, i + 2)
                    if later(i, 0):
                        pe.wait_ge(v_ready, i + 1)
                    for s in range(U):
                        ins = nc.tensor.transpose(xnT_ps[:, s * P:(s + 1) * P], xn[:, s, :], ident[:])
                    ins.then_inc(xnT_made, 1)
                if second:
                    pe.wait_ge(oT_ready, i)
                    for s in range(U):
                        M(ao_ps[:, s * D:(s + 1) * D], oT[:, s * P:(s + 1) * P], wout_sb[:], start=True, stop=False)
                        ins = M(ao_ps[:, s * D:(s + 1) * D], ones_bf[0:96, :], bias_bf[0:96, BIAS_N + D:BIAS_N + 2 * D],
                                start=False, stop=True)
                    ins.then_inc(ao_made, 1)
                if norm:
                    pe.wait_ge(xnT_ready, i + 2)
                    if later(i, 0):
                        pe.wait_ge(act_qk, 4 * i + 4)
                    M(qk_ps[:, 0:W], wqkv_sb[:, 0:D], xnT[:], start=True, stop=True)
                    M(qk_ps[:, W:2 * W], wqkv_sb[:, D:2 * D], xnT[:], start=True, stop=True).then_inc(qk_made, 1)

            skewed(pe, step)

            pe.wait_ge(cum_ready, UNITS)
            pe.wait_ge(rank_ready, UNITS)
            M(cnt_ps, ones_bf[:], cum[:, (UNITS + 1) % 2, :], start=True, stop=True).then_inc(cnt_made, 1)
            pe.wait_ge(tab_step, TAB_STEPS)
            for q in range(2):
                ins = M(tab_ps[0:1, q * P:(q + 1) * P], tab[:, q:q + 1], ident[:], start=True, stop=True)
            ins.then_inc(tab_made, 1)
            pe.wait_ge(tab_ready, 2)
            pe.wait_ge(experts_in, 16 * 12)
            pe.wait_ge(sel_ready, 1)
            pe.wait_ge(expert_bias_ready, 1)

            def trans_x(t, r):
                j = t * R + r
                pe.wait_ge(xs_in[r % R], lap(t, r) * 16)
                if later(j, 2):
                    pe.wait_ge(xT_ready, j - 1)
                nc.tensor.transpose(xT_ps[r % 2], xs[:, r % R, 0:D], ident[:]).then_inc(xT_made, 1)

            def experts(t):
                _, values = nc.values_load_multi_w_load_instructions(tab_e[0:1, bass.ds(t * R, R + 2)], engines=(mybir.EngineType.PE,),
                                              min_val=0, max_val=E - 1,
                                              skip_runtime_bounds_check_because="VectorE keeps them in 0 .. E - 1")
                return {k - 2: v for k, v in enumerate(values)}

            def gate_up(t, r, e):
                j = t * R + r
                pe.wait_ge(xT_ready, j + 1)
                if later(j, 2):
                    pe.wait_ge(hh_ready, j - 1)
                M(gu_ps[r % 2][:], xT[:, r % R, :], wgu_sb[:, bass.ds(e * (2 * FF), 2 * FF)], start=True, stop=False)
                M(gu_ps[r % 2][:], sel[:, bass.ds(e, 1), :].rearrange("p a t -> p (a t)"), bias_bf[:, 0:2 * FF],
                  start=False, stop=True).then_inc(gu_made, 1)

            def trans_h(t, r):
                j = t * R + r
                pe.wait_ge(hh_ready, j + 1)
                if later(j, 2):
                    pe.wait_ge(hT_ready, j - 1)
                for q in range(2):
                    ins = nc.tensor.transpose(hT_ps[r % 2][:, q * P:(q + 1) * P], hh[:, r % 2, q * P:(q + 1) * P], ident[:])
                ins.then_inc(hT_made, 1)

            def down(t, r, e):
                j = t * R + r
                pe.wait_ge(hT_ready, j + 1)
                if later(j, 2):
                    pe.wait_ge(y_ready[(r - 2) % R], lap(t, r - 2))
                for q in range(2):
                    M(y_ps[r % 2], hT[:, r % 2, q * P:(q + 1) * P], wd_sb[:, bass.ds(e * (2 * D) + q * D, D)],
                      start=(q == 0), stop=False)
                M(y_ps[r % 2], sel[:, bass.ds(e, 1), :].rearrange("p a t -> p (a t)"), bias_bf[:, 2 * FF:BIAS_N],
                  start=False, stop=True).then_inc(y_made, 1)

            def estep(t, r, full, e):
                if full or r + 1 < TILES:
                    trans_x(t, r + 1)
                if full or r < TILES:
                    gate_up(t, r, e[r])
                if full or 0 <= r - 1 < TILES:
                    trans_h(t, r - 1)
                if full or 0 <= r - 2 < TILES:
                    down(t, r - 2, e[r - 2])

            trans_x(0, 0)
            e = experts(0)
            for j in range(R):
                estep(0, j, False, e)
            with pe.Fori(1, TILES // R - 1) as t:
                e = experts(t)
                for r in range(R):
                    estep(t, r, True, e)
            e = {k + TILES - R: v for k, v in experts(TILES // R - 1).items()}
            for j in range(TILES - R, TILES + 2):
                estep(0, j, False, e)


def kernel(**inputs):
    import numpy as np
    import concourse.bacc as bacc
    from concourse.bass_utils import run_bass_kernel_spmd

    a = {k: np.ascontiguousarray(v) for k, v in inputs.items()}
    b_qkv = a["L0_attn_b_qkv"]
    attn_bias = np.zeros((E, 2 * D), np.float32)
    attn_bias[0, :D] = b_qkv[2 * D:]
    attn_bias[0, D:] = a["L0_attn_b_out"]
    arrays = {
        "ids": np.ascontiguousarray(a["x"].T).view(np.uint32),
        "wt": np.ascontiguousarray(a["L0_tok_W"].T),
        "rows": np.concatenate([a["L0_tok_b"], b_qkv[2 * D:], a["L0_attn_b_out"], a["L0_attn_ln_g"],
                                a["L0_attn_ln_b"], a["L0_ffn_bgate"]]),
        "bqk": np.ascontiguousarray(b_qkv[:2 * D].reshape(2, D).T),
        "decay": np.ascontiguousarray(np.broadcast_to(a["L0_attn_decay_logits"][:, None], (HEADS, HD)).reshape(D, 1)),
        "wqkv": a["L0_attn_W_qkv"],
        "wout": np.ascontiguousarray(a["L0_attn_W_out"].reshape(HEADS // 2, 2, HD, D).transpose(1, 0, 2, 3).reshape(D, D)),
        "wgate": a["L0_ffn_Wgate"],
        "wgu": np.ascontiguousarray(np.concatenate([a["L0_ffn_Wg"], a["L0_ffn_Wu"]], axis=2).transpose(1, 0, 2)
                                    .reshape(P, E * 2 * FF)),
        "wd": np.ascontiguousarray(a["L0_ffn_Wd"].reshape(E, 2, P, D).transpose(2, 0, 1, 3).reshape(P, E * 2 * D)),
        "ebias": np.concatenate([a["L0_ffn_bg"], a["L0_ffn_bu"], a["L0_ffn_bd"], attn_bias], axis=1),
    }
    nc = bacc.Bacc("TRN2", target_bir_lowering=False, num_devices=1)
    args = [nc.dram_tensor(k, v.shape, mybir.dt.from_np(v.dtype), kind="ExternalInput").ap() for k, v in arrays.items()]
    args.append(nc.dram_tensor("out", (TOK, D), F32, kind="ExternalOutput").ap())
    build(nc, *args)
    r = run_bass_kernel_spmd(nc, [arrays], core_ids=[0])
    return r.results[0]["out"].reshape(SEQS, P, D)
```
